# Optimizing a Trainium2 kernel written in Bass

```python
import numpy as np
import jax
import jax.numpy as jnp

def _softmax(x, axis=-1):
    return jax.nn.softmax(x, axis=axis)

def _gelu(x):
    return jax.nn.gelu(x, approximate=True)

def _silu(x):
    return jax.nn.silu(x)

def _sigmoid(x):
    return jax.nn.sigmoid(x)

def _layernorm(x, axis=-1, eps=1e-05):
    m = jnp.mean(x, axis=axis, keepdims=True)
    v = jnp.var(x, axis=axis, keepdims=True)
    return (x - m) / jnp.sqrt(v + eps)

def _scatter_add(tgt, idx, src, axis=0):
    return tgt.at[idx].add(src)

def _segment_sum(src, seg, n):
    return jax.ops.segment_sum(src, seg, n)
kernel_name = 'mk_adj_preln_d1_adj_r2_d83e45'

def setup_inputs(seed: int=0):
    np.random.seed(seed)
    _w = jnp.asarray

    def _rec_inputs():
        import jax
        import jax.numpy as jnp
        _gk = jax.random.key(seed)
        x = -0.0005207 + 1.001 * jax.random.normal(jax.random.fold_in(_gk, 1), (16, 512, 128), jnp.float32)
        _a = jax.random.bernoulli(jax.random.fold_in(_gk, 2), 0.015625, (16, 512, 512))
        _a = jnp.logical_or(_a, jnp.swapaxes(_a, -1, -2))
        _a = jnp.logical_or(_a, jnp.eye(512, dtype=bool))
        _af = _a.astype(jnp.float32)
        _af = _af * jax.random.uniform(jax.random.fold_in(_gk, 3), (16, 512, 512), jnp.float32, 0.05, 1)
        adj = _af
        return (x, adj)
    x, adj = _rec_inputs()

    def _L0_gnn_setup():
        import jax, jax.numpy as jnp
        import numpy as np
        B, N, F = (8, 512, 128)
        OUT, REL = (128, 16)
        NADJ = 7
        key = jax.random.key(seed)
        k0, k1, k2, k3, k4 = jax.random.split(key, 5)
        features = jax.random.normal(k0, (B, N, F), dtype=jnp.float32)
        A1 = jax.random.uniform(k1, (B, N, N), dtype=jnp.float32)
        A2 = jax.random.uniform(k2, (B, N, N), dtype=jnp.float32)
        W = jax.random.normal(k3, (NADJ, F + REL, OUT), dtype=jnp.float32) * 0.05
        W_edges = jnp.ones((NADJ, REL), dtype=jnp.float32)
        b = jax.random.uniform(k4, (N, OUT), dtype=jnp.float32, minval=-0.05, maxval=0.05)
        return {'features': features, 'A1': A1, 'A2': A2, 'W': W, 'W_edges': W_edges, 'b': b}
    _L0_gnn_all = _L0_gnn_setup()
    _L0_gnn_in = {k: v for k, v in _L0_gnn_all.items() if k in ('W', 'W_edges', 'b')}
    del _L0_gnn_all
    return {'x': x, 'adj': adj, 'L0_gnn_W': _L0_gnn_in['W'], 'L0_gnn_W_edges': _L0_gnn_in['W_edges'], 'L0_gnn_b': _L0_gnn_in['b']}

def reference(x, adj, L0_gnn_W, L0_gnn_W_edges, L0_gnn_b):
    import jax
    import jax.numpy as jnp

    def _L0_gnn_ref(features, A1, A2, W, W_edges, b):
        import jax, jax.numpy as jnp
        import numpy as np
        B, N, F = (8, 512, 128)
        OUT, REL = (128, 16)
        NADJ = 7
        eye = jnp.zeros_like(A1) + jnp.eye(N, dtype=A1.dtype)
        shifted = jnp.roll(eye, 1, axis=0)
        A_fwd = [A1, A2, shifted]
        A_list = A_fwd + [jnp.swapaxes(a, 1, 2) for a in A_fwd]
        A_list.append(eye)
        A = jnp.stack(A_list, axis=0)
        HW = jnp.einsum('bnf,rfo->rbno', features, W[:, :F]) + jnp.einsum('rd,rdo->ro', W_edges, W[:, F:])[:, None, None, :]
        AHW = jnp.einsum('rbnm,rbmo->rbno', A, HW)
        out = jnp.max(AHW, axis=0) + b
        return out
    h = jnp.maximum(_layernorm(x, axis=-1), 0.0)
    x = x + _L0_gnn_ref(h, adj, adj, L0_gnn_W, L0_gnn_W_edges, L0_gnn_b)
    return x

_drawn_inputs = setup_inputs


def setup_inputs(seed=0):
    import zlib

    import numpy as np

    out = dict(_drawn_inputs(seed))
    spreads = {'L0_gnn_W_edges': (1.0, 0.2)}
    factors = {'L0_gnn_b': 7.198}
    for name, (base, spread) in spreads.items():
        noise = np.random.default_rng([zlib.crc32(name.encode()), seed]).standard_normal(out[name].shape)
        drawn = base * np.exp(spread * noise) if base else spread * noise
        out[name] = jnp.asarray(drawn.astype(out[name].dtype))
    for name, factor in factors.items():
        out[name] = (out[name] * factor).astype(out[name].dtype)
    return out
```

```python
from contextlib import ExitStack

import concourse.bass as bass
from concourse import mybir

ALU = mybir.AluOpType
ACT = mybir.ActivationFunctionType
F32 = mybir.dt.float32
F32R = mybir.dt.float32r
EPS = 1e-5
P = 128

H_RELS = (2, 5, 6)
AT_RELS = (3, 4)
A_RELS = (0, 1)
ORDER = H_RELS + AT_RELS + A_RELS
NPROD = len(ORDER)
NPB = 3


def gnn_kernel(nc: bass.Bass, x: bass.AP, adj: bass.AP, W: bass.AP, W_edges: bass.AP, bias: bass.AP, out: bass.AP):
    B, N, F = x.shape
    R, FE, O = W.shape
    REL = FE - F
    C = N // P
    assert F == P and O == P and N == C * P and N <= 512 and R == NPROD and B % 2 == 0 and B >= 6

    x_dram = x.rearrange("b (c p) f -> b p c f", p=P)
    adj_dram = adj.rearrange("b (c p) m -> b p c m", p=P)
    out_dram = out.rearrange("b (c p) f -> b p c f", p=P)
    bias_dram = bias.rearrange("(c p) f -> p c f", p=P)

    with ExitStack() as ctx:
        def sb(name, shape, dt=F32):
            return ctx.enter_context(nc.sbuf_tensor(name, shape, dt))

        def bank(name):
            return ctx.enter_context(nc.psum_tensor(name, [P, 512], F32))

        def sem(name):
            return ctx.enter_context(nc.semaphore(name))

        x_sb = [sb(f"x_sb{i}", [P, C, F]) for i in range(2)]
        adj_sb = [sb(f"adj_sb{i}", [P, C, N]) for i in range(2)]
        norm = [sb(f"norm{i}", [P, C, F]) for i in range(2)]
        h_hi = [sb(f"h_hi{i}", [P, C, F], F32R) for i in range(2)]
        h_lo = [sb(f"h_lo{i}", [P, C, F], F32R) for i in range(2)]
        hT_hi = [sb(f"hT_hi{i}", [P, N], F32R) for i in range(2)]
        hT_lo = [sb(f"hT_lo{i}", [P, N], F32R) for i in range(2)]
        a_hi = [sb(f"a_hi{i}", [P, C, N], F32R) for i in range(2)]
        a_lo = [sb(f"a_lo{i}", [P, C, N], F32R) for i in range(2)]
        aT_hi = [sb(f"aT_hi{i}", [P, C, N], F32R) for i in range(2)]
        aT_lo = [sb(f"aT_lo{i}", [P, C, N], F32R) for i in range(2)]
        x_bias = [sb(f"x_bias{i}", [P, C, F]) for i in range(2)]
        sums = [sb(f"sums{i}", [P, 2, C]) for i in range(2)]
        sum_parts = [sb(f"sum_parts{i}", [P, C, 2, 2, 2]) for i in range(2)]
        sumsT = [sb(f"sumsT{i}", [8, N], F32R) for i in range(2)]
        o_sb = [sb(f"o_sb{i}", [P, C, O]) for i in range(2)]
        stats = sb("stats", [P, C, 6])
        mean_var = sb("mean_var", [P, C, 2])
        var_eps = sb("var_eps", [P, C])
        std = sb("std", [P, C])
        wait_carrier = sb("wait_carrier", [P, 1])
        rstd = sb("rstd", [P, C])
        gT_hi = sb("gT_hi", [P, N], F32R)
        gT_lo = sb("gT_lo", [P, N], F32R)
        g_hi = sb("g_hi", [P, N], F32R)
        g_lo = sb("g_lo", [P, N], F32R)
        best = [sb(f"best{i}", [P, N]) for i in range(2)]
        ident = sb("ident", [P, P])
        zero = sb("zero", [P, P])
        w_sb = sb("w_sb", [P, R, O])
        w_hi = sb("w_hi", [P, R, O], F32R)
        w_lo = sb("w_lo", [P, R, O], F32R)
        w_rel = sb("w_rel", [REL, R, O])
        w_edge = sb("w_edge", [REL, R])
        bias_sb = sb("bias_sb", [P, C, F])
        c_col = sb("c_col", [P, R])
        c_hi = sb("c_hi", [P, R], F32R)
        c_lo = sb("c_lo", [P, R])
        c_parts = sb("c_parts", [P, 4, 2, 2, 2])
        c_rows = sb("c_rows", [8, 4, O], F32R)

        bank_t = [bank(f"bank_t{i}") for i in range(2)]
        bank_gT = bank("bank_gT")
        bank_g = bank("bank_g")
        bank_p = [bank(f"bank_p{i}") for i in range(NPB)]
        bank_m = bank("bank_m")

        x_in = [sem(f"x_in{i}") for i in range(2)]
        adj_in = [sem(f"adj_in{i}") for i in range(2)]
        w_in = sem("w_in")
        stored = [sem(f"stored{i}") for i in range(2)]
        ident_zeroed = sem("ident_zeroed")
        ident_ready = sem("ident_ready")
        w_hi_ready = sem("w_hi_ready")
        w_lo_ready = sem("w_lo_ready")
        c_psum = sem("c_psum")
        c_step = sem("c_step")
        crow_psum = sem("crow_psum")
        crow_ready = sem("crow_ready")
        stats_done = sem("stats_done")
        aggr_done = sem("aggr_done")
        vareps_ready = sem("vareps_ready")
        std_ready = sem("std_ready")
        rstd_ready = sem("rstd_ready")
        norm_ready = sem("norm_ready")
        hhi_ready = sem("hhi_ready")
        hlo_ready = sem("hlo_ready")
        xb_ready = sem("xb_ready")
        ahi_ready = sem("ahi_ready")
        alo_ready = sem("alo_ready")
        aT_psum = sem("aT_psum")
        aThi_ready = sem("aThi_ready")
        aTlo_ready = sem("aTlo_ready")
        hT_psum = sem("hT_psum")
        hThi_ready = sem("hThi_ready")
        hTlo_ready = sem("hTlo_ready")
        sumhi_ready = sem("sumhi_ready")
        sumlo_ready = sem("sumlo_ready")
        sumsT_psum = sem("sumsT_psum")
        sumsT_ready = sem("sumsT_ready")
        gT_psum = sem("gT_psum")
        gThi_ready = sem("gThi_ready")
        gTlo_ready = sem("gTlo_ready")
        g_psum = sem("g_psum")
        ghi_ready = sem("ghi_ready")
        glo_ready = sem("glo_ready")
        prod_psum = sem("prod_psum")
        best_begun = sem("best_begun")
        best_done = sem("best_done")
        fin_psum = sem("fin_psum")
        out_ready = sem("out_ready")

        FIRST, LAST = 2, B - 2

        def pipeline(engine_type, prologue, step):
            prologue()
            for b in range(FIRST):
                step(b, b % 2, b == 0, False)
            with nc.Fori(FIRST // 2, LAST // 2, engines=[engine_type], hint_back_edge=True) as pair:
                for q in range(2):
                    step(pair * 2 + q, q, False, False)
            for b in range(LAST, B):
                step(b, b % 2, False, b == B - 1)

        block = ctx.enter_context(nc.Block())

        @block.sync
        def _(sp):
            def load(b, q, again):
                if again:
                    sp.wait_ge(xb_ready, b - 1)
                    sp.wait_ge(norm_ready, b - 1)
                sp.dma_start(x_sb[q][:, :, :], x_dram[b]).then_inc(x_in[q], 16)
                if again:
                    sp.wait_ge(aT_psum, (b - 1) * C)
                    sp.wait_ge(alo_ready, (b - 1) * C)
                sp.dma_start(adj_sb[q][:, :, :], adj_dram[b]).then_inc(adj_in[q], 16)

            def store(b, q):
                sp.wait_ge(out_ready, b + 1)
                sp.dma_start(out_dram[b], o_sb[q][:, :, :]).then_inc(stored[q], 16)

            def prologue():
                load(0, 0, False)
                sp.dma_start(w_edge[:, :], W_edges.rearrange("r d -> d r"),
                             allow_slow_non_contiguous=True).then_inc(w_in, 16)
                sp.dma_start(w_rel[:, :, :], W[:, F:, :].rearrange("r d o -> d r o")).then_inc(w_in, 16)
                sp.dma_start(w_sb[:, :, :], W[:, :F, :].rearrange("r f o -> f r o")).then_inc(w_in, 16)
                sp.dma_start(bias_sb[:, :, :], bias_dram).then_inc(w_in, 16)
                load(1, 1, False)

            def step(b, q, first, last):
                if isinstance(b, int):
                    if b + 2 < B:
                        load(b + 2, q, True)
                else:
                    load(b + 2, q, True)
                if not first:
                    store(b - 1, 1 - q)

            prologue()
            pipeline(mybir.EngineType.SP, lambda: None, step)
            store(B - 1, (B - 1) % 2)
            for q in range(2):
                sp.wait_ge(stored[q], 16 * (B // 2))

        @block.gpsimd
        def _(pool):
            def prepare(b, q, again):
                if again:
                    pool.wait_ge(hT_psum, b - 1)
                    pool.wait_ge(hlo_ready, b - 1)
                    pool.wait_ge(out_ready, b - 1)
                pool.wait_ge(rstd_ready, b + 1)
                nc.gpsimd.tensor_tensor(x_bias[q][:, :, :], x_sb[q][:, :, :], bias_sb[:, :, :],
                                        ALU.add).then_inc(xb_ready, 1)
                for c in range(C):
                    last = nc.gpsimd.tensor_scalar(norm[q][:, c, :], x_sb[q][:, c, :], mean_var[:, c, 0:1],
                                                   rstd[:, c:c + 1], ALU.subtract, ALU.mult)
                last.then_inc(norm_ready, 1)
                if again:
                    pool.wait_ge(gT_psum, b - 1)
                for c in range(C):
                    pool.wait_ge(ahi_ready, b * C + c + 1)
                    nc.gpsimd.tensor_tensor(a_lo[q][:, c, :], adj_sb[q][:, c, :], a_hi[q][:, c, :].bitcast(F32),
                                            ALU.subtract).then_inc(alo_ready, 1)

            def prologue():
                nc.gpsimd.memset(ident[:, :], 0.0).then_inc(ident_zeroed, 1)
                pool.wait_ge(ident_zeroed, 1)
                nc.gpsimd.affine_select(out=ident[:, :], in_=ident[:, :], compare_op=ALU.not_equal, fill=1.0,
                                        base=0, pattern=[[-1, P]], channel_multiplier=1).then_inc(ident_ready, 1)
                pool.wait_ge(w_in, 64)
                pool.wait_ge(x_in[0], 16)
                prepare(0, 0, False)

            def step(b, q, first, last):
                if not last:
                    prepare(b + 1, 1 - q, not first)

            pipeline(mybir.EngineType.Pool, prologue, step)

        @block.scalar
        def _(act):
            def std_of(b):
                act.wait_ge(vareps_ready, b + 1)
                nc.scalar.activation(std[:, :], var_eps[:, :], ACT.Sqrt).then_inc(std_ready, 1)

            def split_adj(b, q, chunks, again):
                for c in chunks:
                    if c == 0:
                        act.wait_ge(adj_in[q], 16 * ((b - q) // 2 + 1) if isinstance(b, int) else (b - q) * 8 + 16)
                        if again:
                            act.wait_ge(gT_psum, b - 1)
                            act.wait_ge(sumlo_ready, b - 1)
                    nc.scalar.activation(a_hi[q][:, c, :], adj_sb[q][:, c, :], ACT.Copy,
                                         accum_out=sums[q][:, 0, c:c + 1]).then_inc(ahi_ready, 1)

            def split_adjT(b, q, k, again):
                act.wait_ge(aT_psum, b * C + k + 1)
                if again and k == 0:
                    act.wait_ge(g_psum, b - 1)
                nc.scalar.activation(aT_hi[q][:, k, :], bank_t[k % 2][:, 0:N], ACT.Copy,
                                     accum_out=sums[q][:, 1, k:k + 1]).then_inc(aThi_ready, 1)

            def split_hT(b, q, again):
                act.wait_ge(hT_psum, b + 1)
                if again:
                    act.wait_ge(prod_psum, (b - 2) * NPROD + len(H_RELS))
                nc.scalar.activation(hT_hi[q][:, :], bank_m[:, 0:N], ACT.Relu).then_inc(hThi_ready, 1)

            def split_gT(b, first):
                act.wait_ge(gT_psum, b + 1)
                if not first:
                    act.wait_ge(prod_psum, b * NPROD - len(A_RELS))
                nc.scalar.activation(gT_hi[:, :], bank_gT[:, 0:N], ACT.Copy).then_inc(gThi_ready, 1)

            def split_g(b, first):
                act.wait_ge(g_psum, b + 1)
                if not first:
                    act.wait_ge(prod_psum, b * NPROD)
                nc.scalar.activation(g_hi[:, :], bank_g[:, 0:N], ACT.Copy).then_inc(ghi_ready, 1)

            def begin_best(b, q, again):
                r = ORDER[0]
                act.wait_ge(prod_psum, b * NPROD + 1)
                if again:
                    act.wait_ge(fin_psum, b - 1)
                nc.scalar.activation(best[q][:, :], bank_p[0][:, 0:N], ACT.Identity,
                                     bias=c_col[:, r:r + 1]).then_inc(best_begun, 1)

            def prologue():
                act.wait_ge(w_in, 64)
                nc.scalar.activation(w_hi[:, :, :], w_sb[:, :, :], ACT.Copy).then_inc(w_hi_ready, 1)
                std_of(0)
                split_adj(0, 0, range(C), False)
                split_adjT(0, 0, 0, False)
                split_adjT(0, 0, 1, False)
                split_hT(0, 0, False)
                split_adjT(0, 0, 2, False)
                split_adjT(0, 0, 3, False)
                act.wait_ge(c_step, 1)

            def step(b, q, first, last):
                nb, nq, again = b + 1, 1 - q, not first
                if not last:
                    std_of(nb)
                    split_adj(nb, nq, range(0, 3), again)
                split_gT(b, first)
                if not last:
                    split_adj(nb, nq, range(3, C), again)
                begin_best(b, q, not first and not (isinstance(b, int) and b < 2))
                if not last:
                    split_adjT(nb, nq, 0, again)
                    split_adjT(nb, nq, 1, again)
                split_g(b, first)
                if not last:
                    split_hT(nb, nq, again)
                    split_adjT(nb, nq, 2, again)
                    split_adjT(nb, nq, 3, again)

            pipeline(mybir.EngineType.Activation, prologue, step)

        @block.vector
        def _(dve):
            def x_landed(b, q):
                dve.wait_ge(x_in[q], 16 * ((b - q) // 2 + 1) if isinstance(b, int) else (b - q) * 8 + 16)

            def layernorm_stats(b, q, first):
                x_landed(b, q)
                if not first:
                    dve.wait_ge(norm_ready, b)
                for c in range(C):
                    last = nc.vector.bn_stats(stats[:, c, :], x_sb[q][:, c, :])
                last.then_inc(stats_done, 1)
                dve.wait_ge(stats_done, b + 1)
                nc.vector.memset(wait_carrier[:, :], 0.0)
                for c in range(C):
                    last = nc.vector.bn_aggr(mean_var[:, c, :], stats[:, c, :])
                last.then_inc(aggr_done, 1)
                dve.wait_ge(aggr_done, b + 1)
                if not first:
                    dve.wait_ge(std_ready, b)
                nc.vector.tensor_scalar(var_eps[:, :], mean_var[:, :, 1], EPS, None, ALU.add).then_inc(vareps_ready, 1)
                dve.wait_ge(std_ready, b + 1)
                nc.vector.reciprocal(rstd[:, :], std[:, :]).then_inc(rstd_ready, 1)

            def split_h(b, q, again):
                dve.wait_ge(norm_ready, b + 1)
                if again:
                    dve.wait_ge(gT_psum, b - 1)
                    dve.wait_ge(g_psum, b - 1)
                nc.vector.tensor_scalar(h_hi[q][:, :, :], norm[q][:, :, :], 0.0, None, ALU.max).then_inc(hhi_ready, 1)
                dve.wait_ge(hhi_ready, b + 1)
                nc.vector.scalar_tensor_tensor(out=h_lo[q][:, :, :], in0=norm[q][:, :, :], scalar=0.0,
                                               in1=h_hi[q][:, :, :].bitcast(F32), op0=ALU.max,
                                               op1=ALU.subtract).then_inc(hlo_ready, 1)

            def lo_adjT(b, q, k):
                dve.wait_ge(aThi_ready, b * C + k + 1)
                nc.vector.tensor_tensor(aT_lo[q][:, k, :], bank_t[k % 2][:, 0:N], aT_hi[q][:, k, :].bitcast(F32),
                                        ALU.subtract).then_inc(aTlo_ready, 1)

            def lo_hT(b, q):
                dve.wait_ge(hThi_ready, b + 1)
                nc.vector.scalar_tensor_tensor(out=hT_lo[q][:, :], in0=bank_m[:, 0:N], scalar=0.0,
                                               in1=hT_hi[q][:, :].bitcast(F32), op0=ALU.max,
                                               op1=ALU.subtract).then_inc(hTlo_ready, 1)

            def lo_gT(b):
                dve.wait_ge(gThi_ready, b + 1)
                nc.vector.tensor_tensor(gT_lo[:, :], bank_gT[:, 0:N], gT_hi[:, :].bitcast(F32),
                                        ALU.subtract).then_inc(gTlo_ready, 1)

            def lo_g(b):
                dve.wait_ge(ghi_ready, b + 1)
                nc.vector.tensor_tensor(g_lo[:, :], bank_g[:, 0:N], g_hi[:, :].bitcast(F32),
                                        ALU.subtract).then_inc(glo_ready, 1)

            def split_sums(b, q, again):
                dve.wait_ge(aThi_ready, (b + 1) * C)
                dve.wait_ge(ahi_ready, (b + 1) * C)
                if again:
                    dve.wait_ge(sumsT_psum, b - 1)
                parts = sum_parts[q]
                s = sums[q][:, :, :].rearrange("p d c -> p c d")
                for copy in range(2):
                    last = nc.vector.tensor_copy(parts[:, :, copy, :, 0].bitcast(F32R), s)
                last.then_inc(sumhi_ready, 1)
                dve.wait_ge(sumhi_ready, b + 1)
                for copy in range(2):
                    last = nc.vector.tensor_tensor(parts[:, :, copy, :, 1], s, parts[:, :, copy, :, 0],
                                                   ALU.subtract)
                last.then_inc(sumlo_ready, 1)

            def copy_sumsT(b, q, again):
                dve.wait_ge(sumsT_psum, b + 1)
                if again:
                    dve.wait_ge(prod_psum, (b - 1) * NPROD)
                nc.vector.tensor_copy(sumsT[q][:, :], bank_m[0:8, 0:N]).then_inc(sumsT_ready, 1)

            def take_best(b, q, i):
                r = ORDER[i]
                dve.wait_ge(prod_psum, b * NPROD + i + 1)
                if i == 1:
                    dve.wait_ge(best_begun, b + 1)
                else:
                    dve.wait_ge(best_done, b * (NPROD - 1) + i - 1)
                if r in H_RELS:
                    op = nc.vector.scalar_tensor_tensor(out=best[q][:, :], in0=bank_p[i % NPB][:, 0:N],
                                                        scalar=c_col[:, r:r + 1], in1=best[q][:, :],
                                                        op0=ALU.add, op1=ALU.max)
                else:
                    op = nc.vector.tensor_tensor(best[q][:, :], bank_p[i % NPB][:, 0:N], best[q][:, :], ALU.max)
                op.then_inc(best_done, 1)

            def finish(b, q, again):
                dve.wait_ge(fin_psum, b + 1)
                dve.wait_ge(xb_ready, b + 1)
                if again:
                    dve.wait_ge(stored[q], 16 * ((b - q) // 2) if isinstance(b, int) else (b - q) * 8)
                nc.vector.tensor_tensor(o_sb[q][:, :, :], bank_m[:, :].rearrange("p (c o) -> p c o", c=C),
                                        x_bias[q][:, :, :], ALU.add).then_inc(out_ready, 1)

            def prologue():
                layernorm_stats(0, 0, True)
                dve.wait_ge(w_hi_ready, 1)
                nc.vector.tensor_tensor(w_lo[:, :, :], w_sb[:, :, :], w_hi[:, :, :].bitcast(F32),
                                        ALU.subtract).then_inc(w_lo_ready, 1)
                split_h(0, 0, False)
                dve.wait_ge(c_psum, 1)
                nc.vector.memset(c_parts[:, :, :, :, :], 0.0)
                nc.vector.tensor_copy(c_col[:, :], bank_g[:, 0:R]).then_inc(c_step, 1)
                dve.wait_ge(c_step, 1)
                nc.vector.tensor_copy(c_hi[:, :], c_col[:, :]).then_inc(c_step, 1)
                dve.wait_ge(c_step, 2)
                nc.vector.tensor_tensor(c_lo[:, :], c_col[:, :], c_hi[:, :].bitcast(F32), ALU.subtract).then_inc(c_step, 1)
                dve.wait_ge(c_step, 3)
                for d, rels in enumerate((A_RELS, AT_RELS)):
                    for copy, part in enumerate((c_hi[:, :].bitcast(F32), c_lo[:, :])):
                        for s in range(2):
                            last = nc.vector.tensor_copy(c_parts[:, 2 * d:2 * d + 2, copy, d, s],
                                                         part[:, rels[0]:rels[0] + 2])
                last.then_inc(c_step, 1)
                lo_adjT(0, 0, 0)
                lo_adjT(0, 0, 1)
                lo_hT(0, 0)
                lo_adjT(0, 0, 2)
                lo_adjT(0, 0, 3)
                split_sums(0, 0, False)
                copy_sumsT(0, 0, False)
                dve.wait_ge(crow_psum, 1)
                nc.vector.tensor_copy(c_rows[:, :, :], bank_g[0:8, :].rearrange("k (r o) -> k r o", r=4)
                                      ).then_inc(crow_ready, 1)

            def step(b, q, first, last):
                nb, nq, again = b + 1, 1 - q, not first
                if not last:
                    layernorm_stats(nb, nq, False)
                lo_gT(b)
                if not first:
                    finish(b - 1, nq, not (isinstance(b, int) and b <= 2))
                if not last:
                    split_h(nb, nq, again)
                take_best(b, q, 1)
                take_best(b, q, 2)
                if not last:
                    lo_adjT(nb, nq, 0)
                    lo_adjT(nb, nq, 1)
                lo_g(b)
                if not last:
                    lo_hT(nb, nq)
                take_best(b, q, 3)
                if not last:
                    lo_adjT(nb, nq, 2)
                take_best(b, q, 4)
                if not last:
                    lo_adjT(nb, nq, 3)
                    split_sums(nb, nq, again)
                take_best(b, q, 5)
                take_best(b, q, 6)
                if not last:
                    copy_sumsT(nb, nq, again)

            pipeline(mybir.EngineType.DVE, prologue, step)
            finish(B - 1, (B - 1) % 2, True)

        @block.tensor
        def _(pe):
            def transpose_adj(b, q, k, first):
                if k == 0:
                    pe.wait_ge(adj_in[q], 16 * ((b - q) // 2 + 1) if isinstance(b, int) else (b - q) * 8 + 16)
                if not (first and k < 2):
                    pe.wait_ge(aTlo_ready, b * C + k - 1)
                for c in range(C):
                    last = nc.tensor.transpose(bank_t[k % 2][:, c * P:(c + 1) * P],
                                               adj_sb[q][:, c, k * P:(k + 1) * P], ident[:, :])
                last.then_inc(aT_psum, 1)

            def transpose_h(b, q, first):
                pe.wait_ge(norm_ready, b + 1)
                if not first:
                    pe.wait_ge(sumsT_ready, b)
                for c in range(C):
                    last = nc.tensor.transpose(bank_m[:, c * P:(c + 1) * P], norm[q][:, c, :], ident[:, :])
                last.then_inc(hT_psum, 1)

            def transpose_sums(b, q):
                pe.wait_ge(sumlo_ready, b + 1)
                pe.wait_ge(hTlo_ready, b + 1)
                for c in range(C):
                    last = nc.tensor.transpose(bank_m[0:8, c * P:(c + 1) * P],
                                               sum_parts[q][:, c, :, :, :].rearrange("p a b c -> p (a b c)"),
                                               ident[:, :])
                last.then_inc(sumsT_psum, 1)

            def transpose_best(b, q):
                pe.wait_ge(best_done, (b + 1) * (NPROD - 1))
                pe.wait_ge(sumsT_ready, b + 2)
                for c in range(C):
                    last = nc.tensor.transpose(bank_m[:, c * P:(c + 1) * P], best[q][:, c * P:(c + 1) * P],
                                               ident[:, :])
                last.then_inc(fin_psum, 1)

            def aggregate_T(b, q, first):
                pe.wait_ge(hlo_ready, b + 1)
                if not first:
                    pe.wait_ge(gTlo_ready, b)
                for c in range(C):
                    pe.wait_ge(ahi_ready, b * C + c + 1)
                    nc.tensor.matmul(bank_gT[:, 0:N], h_hi[q][:, c, :], a_hi[q][:, c, :], start=(c == 0), stop=False)
                    nc.tensor.matmul(bank_gT[:, 0:N], h_lo[q][:, c, :], a_hi[q][:, c, :], start=False, stop=False)
                for c in range(C):
                    pe.wait_ge(alo_ready, b * C + c + 1)
                    last = nc.tensor.matmul(bank_gT[:, 0:N], h_hi[q][:, c, :], a_lo[q][:, c, :],
                                            start=False, stop=(c == C - 1))
                last.then_inc(gT_psum, 1)

            def aggregate(b, q, first, half):
                if half == 0 and not first:
                    pe.wait_ge(glo_ready, b)
                for k in range(half * C // 2, (half + 1) * C // 2):
                    pe.wait_ge(aTlo_ready, b * C + k + 1)
                    nc.tensor.matmul(bank_g[:, 0:N], h_hi[q][:, k, :], aT_hi[q][:, k, :], start=(k == 0), stop=False)
                    nc.tensor.matmul(bank_g[:, 0:N], h_lo[q][:, k, :], aT_hi[q][:, k, :], start=False, stop=False)
                    last = nc.tensor.matmul(bank_g[:, 0:N], h_hi[q][:, k, :], aT_lo[q][:, k, :],
                                            start=False, stop=(k == C - 1))
                if half == 1:
                    last.then_inc(g_psum, 1)

            def product(b, q, i, first):
                r = ORDER[i]
                dst = bank_p[i % NPB][:, 0:N]
                if i >= NPB:
                    if i == NPB:
                        pe.wait_ge(best_begun, b + 1)
                    else:
                        pe.wait_ge(best_done, b * (NPROD - 1) + i - NPB)
                elif not first:
                    pe.wait_ge(best_done, b * (NPROD - 1))
                if r in H_RELS:
                    pe.wait_ge(hTlo_ready, b + 1)
                    hi, lo = hT_hi[q], hT_lo[q]
                elif r in AT_RELS:
                    pe.wait_ge(gTlo_ready, b + 1)
                    hi, lo = gT_hi, gT_lo
                else:
                    pe.wait_ge(glo_ready, b + 1)
                    hi, lo = g_hi, g_lo
                nc.tensor.matmul(dst, w_hi[:, r, :], hi[:, :], start=True, stop=False)
                nc.tensor.matmul(dst, w_lo[:, r, :], hi[:, :], start=False, stop=False)
                last = nc.tensor.matmul(dst, w_hi[:, r, :], lo[:, :], start=False, stop=(r in H_RELS))
                if r not in H_RELS:
                    pe.wait_ge(sumsT_ready, b + 1)
                    k = (A_RELS + AT_RELS).index(r)
                    last = nc.tensor.matmul(dst, c_rows[:, k, :], sumsT[q][:, :], start=False, stop=True)
                last.then_inc(prod_psum, 1)

            def prologue():
                pe.wait_ge(ident_ready, 1)
                transpose_adj(0, 0, 0, True)
                transpose_adj(0, 0, 1, True)
                pe.wait_ge(w_in, 64)
                for r in range(R):
                    last = nc.tensor.matmul(bank_g[:, r:r + 1], w_rel[:, r, :], w_edge[:, r:r + 1],
                                            start=True, stop=True)
                last.then_inc(c_psum, 1)
                transpose_h(0, 0, True)
                transpose_adj(0, 0, 2, True)
                transpose_adj(0, 0, 3, True)
                pe.wait_ge(c_step, 4)
                for k in range(4):
                    last = nc.tensor.transpose(bank_g[0:8, k * P:(k + 1) * P],
                                               c_parts[:, k, :, :, :].rearrange("p a b c -> p (a b c)"), ident[:, :])
                last.then_inc(crow_psum, 1)
                transpose_sums(0, 0)
                pe.wait_ge(w_lo_ready, 1)
                pe.wait_ge(crow_ready, 1)

            def step(b, q, first, last):
                nb, nq = b + 1, 1 - q
                aggregate_T(b, q, first)
                if not first:
                    transpose_best_of_previous(b, nq)
                for i in range(3):
                    product(b, q, i, first)
                if not last:
                    transpose_adj(nb, nq, 0, False)
                aggregate(b, q, first, 0)
                if not last:
                    transpose_adj(nb, nq, 1, False)
                aggregate(b, q, first, 1)
                if not last:
                    if not first:
                        pe.wait_ge(out_ready, b)
                    transpose_h(nb, nq, False)
                product(b, q, 3, first)
                if not last:
                    transpose_adj(nb, nq, 2, False)
                product(b, q, 4, first)
                if not last:
                    transpose_adj(nb, nq, 3, False)
                product(b, q, 5, first)
                product(b, q, 6, first)
                if not last:
                    transpose_sums(nb, nq)

            def transpose_best_of_previous(b, nq):
                pe.wait_ge(best_done, b * (NPROD - 1))
                pe.wait_ge(sumsT_ready, b + 1)
                for c in range(C):
                    last = nc.tensor.transpose(bank_m[:, c * P:(c + 1) * P], best[nq][:, c * P:(c + 1) * P],
                                               ident[:, :])
                last.then_inc(fin_psum, 1)

            pipeline(mybir.EngineType.PE, prologue, step)
            transpose_best_of_previous_last = (B - 1) % 2
            pe.wait_ge(best_done, B * (NPROD - 1))
            pe.wait_ge(out_ready, B - 1)
            for c in range(C):
                last = nc.tensor.transpose(bank_m[:, c * P:(c + 1) * P],
                                           best[transpose_best_of_previous_last][:, c * P:(c + 1) * P], ident[:, :])
            last.then_inc(fin_psum, 1)


_INS = ['x', 'adj', 'L0_gnn_W', 'L0_gnn_W_edges', 'L0_gnn_b']
_OUTS = [((16, 512, 128), 'float32')]


def kernel(**inputs):
    import numpy as _np
    import concourse.bacc as _bacc
    from concourse import mybir as _mybir
    from concourse.bass_utils import run_bass_kernel_spmd as _run

    nc = _bacc.Bacc("TRN2", target_bir_lowering=False, num_devices=1)
    arrays, args = {}, []
    for name in _INS:
        a = _np.ascontiguousarray(inputs[name])
        arrays[f"in_{name}_dram"] = a
        args.append(nc.dram_tensor(f"in_{name}_dram", a.shape, _mybir.dt.from_np(a.dtype), kind="ExternalInput").ap())
    for i, (shape, dtype) in enumerate(_OUTS):
        dt = _mybir.dt.from_np(_np.dtype(dtype))
        args.append(nc.dram_tensor(f"out_{i}_dram", shape, dt, kind="ExternalOutput").ap())
    gnn_kernel(nc, *args)
    r = _run(nc, [arrays], core_ids=[0])
    return r.results[0]["out_0_dram"]
```

```python
from contextlib import ExitStack

import concourse.bass as bass
from concourse import mybir

ALU = mybir.AluOpType
ACT = mybir.ActivationFunctionType
F32 = mybir.dt.float32
F32R = mybir.dt.float32r
EPS = 1e-5
P = 128

H_RELS = (2, 5, 6)
AT_RELS = (3, 4)
A_RELS = (0, 1)
ORDER = H_RELS + AT_RELS + A_RELS
NPROD = len(ORDER)
NPB = 4
ORDER_A = A_RELS + AT_RELS
POOL_CHUNKS = 2


def gnn_kernel(nc: bass.Bass, x: bass.AP, xT: bass.AP, adj: bass.AP, adjT: bass.AP, W: bass.AP,
               W_edgesT: bass.AP, biasT: bass.AP, outT: bass.AP):
    B, N, F = x.shape
    R, FE, O = W.shape
    REL = FE - F
    C = N // P
    assert F == P and O == P and N == C * P and N <= 512 and R == NPROD and B % 2 == 0 and B >= 6

    x_dram = x.rearrange("b (c p) f -> b p c f", p=P)
    adj_dram = adj.rearrange("b (c p) m -> b p c m", p=P)
    adjT_dram = adjT.rearrange("b (c p) n -> b p c n", p=P)

    with ExitStack() as ctx:
        def sb(name, shape, dt=F32):
            return ctx.enter_context(nc.sbuf_tensor(name, shape, dt))

        def pair(name, shape, dt=F32):
            return [sb(f"{name}{i}", shape, dt) for i in range(2)]

        def bank(name):
            return ctx.enter_context(nc.psum_tensor(name, [P, 512], F32))

        def sem(name):
            return ctx.enter_context(nc.semaphore(name))

        x_sb = pair("x_sb", [P, C, F])
        xT_sb = pair("xT_sb", [P, N])
        adj_sb = pair("adj_sb", [P, C, N])
        adjT_sb = pair("adjT_sb", [P, C, N])
        norm = pair("norm", [P, C, F])
        h_hi = pair("h_hi", [P, C, F], F32R)
        h_lo = pair("h_lo", [P, C, F], F32R)
        hT_hi = pair("hT_hi", [P, N], F32R)
        hT_lo = pair("hT_lo", [P, N], F32R)
        a_hi = pair("a_hi", [P, C, N], F32R)
        a_lo = pair("a_lo", [P, C, N], F32R)
        aT_hi = pair("aT_hi", [P, C, N], F32R)
        aT_lo = pair("aT_lo", [P, C, N], F32R)
        x_bias = pair("x_bias", [P, N])
        sums = pair("sums", [P, 2, C])
        sum_parts = pair("sum_parts", [P, C, 2, 2, 2])
        sumsT = pair("sumsT", [8, N], F32R)
        best = pair("best", [P, N])
        o_sb = pair("o_sb", [P, N])
        stats = sb("stats", [P, C, 6])
        mean_var = sb("mean_var", [P, C, 2])
        var_eps = sb("var_eps", [P, C])
        std = sb("std", [P, C])
        rstd = sb("rstd", [P, C])
        wait_carrier = sb("wait_carrier", [P, 1])
        gT_hi = sb("gT_hi", [P, N], F32R)
        gT_lo = sb("gT_lo", [P, N], F32R)
        g_hi = sb("g_hi", [P, N], F32R)
        g_lo = sb("g_lo", [P, N], F32R)
        ident = sb("ident", [P, P])
        w_sb = sb("w_sb", [P, R, O])
        w_hi = sb("w_hi", [P, R, O], F32R)
        w_lo = sb("w_lo", [P, R, O], F32R)
        w_rel = sb("w_rel", [REL, R, O])
        w_edge = sb("w_edge", [REL, R])
        bias_sb = sb("bias_sb", [P, N])
        c_col = sb("c_col", [P, R])
        c_hi = sb("c_hi", [P, R], F32R)
        c_lo = sb("c_lo", [P, R])
        c_parts = sb("c_parts", [P, 4, 2, 2, 2])
        c_rows = sb("c_rows", [8, 4, O], F32R)

        bank_gT = bank("bank_gT")
        bank_g = bank("bank_g")
        bank_h = bank("bank_h")
        bank_s = bank("bank_s")
        bank_p = [bank(f"bank_p{i}") for i in range(NPB)]

        x_in = [sem(f"x_in{i}") for i in range(2)]
        xT_in = [sem(f"xT_in{i}") for i in range(2)]
        adj_in = [sem(f"adj_in{i}") for i in range(2)]
        adjT_in = [sem(f"adjT_in{i}") for i in range(2)]
        stored = [sem(f"stored{i}") for i in range(2)]
        adj0_in = [sem(f"adj0_in{c}") for c in range(C)]
        wrel_in = sem("wrel_in")
        w_in = sem("w_in")
        bias_in = sem("bias_in")
        ident_zeroed = sem("ident_zeroed")
        ident_ready = sem("ident_ready")
        w_hi_ready = sem("w_hi_ready")
        w_lo_ready = sem("w_lo_ready")
        c_psum = sem("c_psum")
        c_step = sem("c_step")
        crow_psum = sem("crow_psum")
        crow_ready = sem("crow_ready")
        stats_done = sem("stats_done")
        aggr_done = sem("aggr_done")
        vareps_ready = sem("vareps_ready")
        std_ready = sem("std_ready")
        rstd_ready = sem("rstd_ready")
        norm_ready = sem("norm_ready")
        hhi_ready = sem("hhi_ready")
        hlo_ready = sem("hlo_ready")
        xb_ready = sem("xb_ready")
        ahi_ready = sem("ahi_ready")
        alo_ready = sem("alo_ready")
        aThi_ready = sem("aThi_ready")
        aTlo_pool = sem("aTlo_pool")
        aTlo_dve = sem("aTlo_dve")
        hT_psum = sem("hT_psum")
        hThi_ready = sem("hThi_ready")
        hTlo_ready = sem("hTlo_ready")
        sumhi_ready = sem("sumhi_ready")
        sumlo_ready = sem("sumlo_ready")
        sumsT_psum = sem("sumsT_psum")
        sumsT_ready = sem("sumsT_ready")
        gT_psum = sem("gT_psum")
        gThi_ready = sem("gThi_ready")
        gTlo_ready = sem("gTlo_ready")
        g_psum = sem("g_psum")
        ghi_ready = sem("ghi_ready")
        glo_ready = sem("glo_ready")
        prod_psum = sem("prod_psum")
        best_begun = sem("best_begun")
        best_done = sem("best_done")
        out_ready = sem("out_ready")

        NBEST = NPROD - 1
        DVE_CHUNKS = C - POOL_CHUNKS
        FIRST, LAST = 2, B - 2

        def landed(b, q, skipped=0):
            return (b - q) * 8 + 16 * (1 - skipped)

        def pipeline(engine_type, step):
            for b in range(FIRST):
                step(b, b % 2, b == 0, False)
            with nc.Fori(FIRST // 2, LAST // 2, engines=[engine_type], hint_back_edge=True) as two:
                for q in range(2):
                    step(two * 2 + q, q, False, False)
            for b in range(LAST, B):
                step(b, b % 2, False, b == B - 1)

        block = ctx.enter_context(nc.Block())

        @block.sync
        def _(sp):
            def load(b, q):
                sp.wait_ge(norm_ready, b - 1)
                sp.dma_start(x_sb[q][:, :, :], x_dram[b]).then_inc(x_in[q], 16)
                sp.wait_ge(alo_ready, (b - 1) * C)
                sp.dma_start(adj_sb[q][:, :, :], adj_dram[b]).then_inc(adj_in[q], 16)
                sp.wait_ge(aTlo_pool, (b - 1) * POOL_CHUNKS)
                sp.wait_ge(aTlo_dve, (b - 1) * DVE_CHUNKS)
                sp.dma_start(adjT_sb[q][:, :, :], adjT_dram[b]).then_inc(adjT_in[q], 16)
                sp.wait_ge(xb_ready, b - 1)
                sp.dma_start(xT_sb[q][:, :], xT[b]).then_inc(xT_in[q], 16)

            def store(b, q):
                sp.wait_ge(out_ready, b + 1)
                sp.dma_start(outT[b], o_sb[q][:, :]).then_inc(stored[q], 16)

            def step(b, q, first, last):
                if not (isinstance(b, int) and b + 2 >= B):
                    load(b + 2, q)
                if not first:
                    store(b - 1, 1 - q)

            sp.dma_start(x_sb[0][:, :, :], x_dram[0]).then_inc(x_in[0], 16)
            for c in range(C):
                sp.dma_start(adj_sb[0][:, c, :], adj_dram[0][:, c, :]).then_inc(adj0_in[c], 16)
            sp.dma_start(w_sb[:, :, :], W[:, :F, :].rearrange("r f o -> f r o")).then_inc(w_in, 16)
            sp.dma_start(w_edge[:, :], W_edgesT).then_inc(wrel_in, 16)
            sp.dma_start(w_rel[:, :, :], W[:, F:, :].rearrange("r d o -> d r o")).then_inc(wrel_in, 16)
            sp.dma_start(adjT_sb[0][:, :, :], adjT_dram[0]).then_inc(adjT_in[0], 16)
            sp.dma_start(xT_sb[0][:, :], xT[0]).then_inc(xT_in[0], 16)
            sp.dma_start(bias_sb[:, :], biasT).then_inc(bias_in, 16)
            sp.dma_start(x_sb[1][:, :, :], x_dram[1]).then_inc(x_in[1], 16)
            sp.dma_start(adj_sb[1][:, :, :], adj_dram[1]).then_inc(adj_in[1], 16)
            sp.dma_start(adjT_sb[1][:, :, :], adjT_dram[1]).then_inc(adjT_in[1], 16)
            sp.dma_start(xT_sb[1][:, :], xT[1]).then_inc(xT_in[1], 16)
            pipeline(mybir.EngineType.SP, step)
            store(B - 1, (B - 1) % 2)
            for q in range(2):
                sp.wait_ge(stored[q], 16 * (B // 2))

        @block.gpsimd
        def _(pool):
            def split_adj_lo(b, q, again):
                if again:
                    pool.wait_ge(gT_psum, b - 1)
                for c in range(C):
                    pool.wait_ge(ahi_ready, b * C + c + 1)
                    nc.gpsimd.tensor_tensor(a_lo[q][:, c, :], adj_sb[q][:, c, :], a_hi[q][:, c, :].bitcast(F32),
                                            ALU.subtract).then_inc(alo_ready, 1)

            def split_adjT_lo(b, q, again):
                if again:
                    pool.wait_ge(g_psum, b - 1)
                for c in range(POOL_CHUNKS):
                    pool.wait_ge(aThi_ready, b * C + c + 1)
                    nc.gpsimd.tensor_tensor(aT_lo[q][:, c, :], adjT_sb[q][:, c, :], aT_hi[q][:, c, :].bitcast(F32),
                                            ALU.subtract).then_inc(aTlo_pool, 1)

            def add_bias(b, q, again):
                pool.wait_ge(xT_in[q], landed(b, q))
                if again:
                    pool.wait_ge(out_ready, b - 1)
                nc.gpsimd.tensor_tensor(x_bias[q][:, :], xT_sb[q][:, :], bias_sb[:, :], ALU.add).then_inc(xb_ready, 1)

            def finish(b, q, again):
                pool.wait_ge(xb_ready, b + 1)
                if again:
                    pool.wait_ge(stored[q], landed(b, q, 1))
                pool.wait_ge(best_done, (b + 1) * NBEST)
                nc.gpsimd.tensor_tensor(o_sb[q][:, :], best[q][:, :], x_bias[q][:, :], ALU.add).then_inc(out_ready, 1)

            def step(b, q, first, last):
                nb, nq, again = b + 1, 1 - q, not first
                if not first:
                    finish(b - 1, nq, not (isinstance(b, int) and b <= 2))
                if not last:
                    split_adj_lo(nb, nq, again)
                    add_bias(nb, nq, again)
                    split_adjT_lo(nb, nq, again)

            nc.gpsimd.memset(ident[:, :], 0.0).then_inc(ident_zeroed, 1)
            pool.wait_ge(ident_zeroed, 1)
            nc.gpsimd.affine_select(out=ident[:, :], in_=ident[:, :], compare_op=ALU.not_equal, fill=1.0,
                                    base=0, pattern=[[-1, P]], channel_multiplier=1).then_inc(ident_ready, 1)
            split_adj_lo(0, 0, False)
            split_adjT_lo(0, 0, False)
            pool.wait_ge(bias_in, 16)
            add_bias(0, 0, False)
            pipeline(mybir.EngineType.Pool, step)
            finish(B - 1, (B - 1) % 2, True)

        @block.scalar
        def _(act):
            def std_of(b):
                act.wait_ge(vareps_ready, b + 1)
                nc.scalar.activation(std[:, :], var_eps[:, :], ACT.Sqrt).then_inc(std_ready, 1)

            def split_adj(b, q, chunks, again):
                for c in chunks:
                    if isinstance(b, int) and b == 0:
                        act.wait_ge(adj0_in[c], 16)
                    elif c == 0:
                        act.wait_ge(adj_in[q], landed(b, q, 1 - q))
                    if again and c == 0:
                        act.wait_ge(gT_psum, b - 1)
                        act.wait_ge(sumlo_ready, b - 1)
                    nc.scalar.activation(a_hi[q][:, c, :], adj_sb[q][:, c, :], ACT.Copy,
                                         accum_out=sums[q][:, 0, c:c + 1]).then_inc(ahi_ready, 1)

            def split_adjT(b, q, again):
                act.wait_ge(adjT_in[q], landed(b, q))
                if again:
                    act.wait_ge(g_psum, b - 1)
                for c in range(C):
                    nc.scalar.activation(aT_hi[q][:, c, :], adjT_sb[q][:, c, :], ACT.Copy,
                                         accum_out=sums[q][:, 1, c:c + 1]).then_inc(aThi_ready, 1)

            def split_h(b, q, again):
                act.wait_ge(norm_ready, b + 1)
                if again:
                    act.wait_ge(g_psum, b - 1)
                nc.scalar.activation(h_hi[q][:, :, :], norm[q][:, :, :], ACT.Relu).then_inc(hhi_ready, 1)

            def split_hT(b, q, again):
                act.wait_ge(hT_psum, b + 1)
                if again:
                    act.wait_ge(prod_psum, (b - 2) * NPROD + len(H_RELS))
                nc.scalar.activation(hT_hi[q][:, :], bank_h[:, 0:N], ACT.Relu).then_inc(hThi_ready, 1)

            def split_gT(b, first):
                act.wait_ge(gT_psum, b + 1)
                if not first:
                    act.wait_ge(prod_psum, b * NPROD - len(A_RELS))
                nc.scalar.activation(gT_hi[:, :], bank_gT[:, 0:N], ACT.Copy).then_inc(gThi_ready, 1)

            def split_g(b, first):
                act.wait_ge(g_psum, b + 1)
                if not first:
                    act.wait_ge(prod_psum, b * NPROD)
                nc.scalar.activation(g_hi[:, :], bank_g[:, 0:N], ACT.Copy).then_inc(ghi_ready, 1)

            def begin_best(b, q, again):
                r = ORDER[0]
                act.wait_ge(prod_psum, b * NPROD + 1)
                if again:
                    act.wait_ge(out_ready, b - 1)
                nc.scalar.activation(best[q][:, :], bank_p[0][:, 0:N], ACT.Identity,
                                     bias=c_col[:, r:r + 1]).then_inc(best_begun, 1)

            def copy_sumsT(b, q, again):
                act.wait_ge(sumsT_psum, b + 1)
                if again:
                    act.wait_ge(prod_psum, (b - 1) * NPROD)
                nc.scalar.activation(sumsT[q][:, :], bank_s[0:8, 0:N], ACT.Copy).then_inc(sumsT_ready, 1)

            def step(b, q, first, last):
                nb, nq, again = b + 1, 1 - q, not first
                if not last:
                    split_adj(nb, nq, range(0, 3), again)
                    std_of(nb)
                split_gT(b, first)
                if not last:
                    split_h(nb, nq, again)
                    split_adj(nb, nq, range(3, C), again)
                begin_best(b, q, not (isinstance(b, int) and b < 2))
                if not last:
                    split_adjT(nb, nq, again)
                split_g(b, first)
                if first:
                    copy_sumsT(0, 0, False)
                if not last:
                    split_hT(nb, nq, again)
                    copy_sumsT(nb, nq, again)

            std_of(0)
            split_adj(0, 0, range(0, 2), False)
            split_h(0, 0, False)
            split_adj(0, 0, range(2, C), False)
            act.wait_ge(w_in, 16)
            nc.scalar.activation(w_hi[:, :, :], w_sb[:, :, :], ACT.Copy).then_inc(w_hi_ready, 1)
            split_hT(0, 0, False)
            split_adjT(0, 0, False)
            act.wait_ge(c_step, 1)
            pipeline(mybir.EngineType.Activation, step)

        @block.vector
        def _(dve):
            def layernorm(b, q, again):
                dve.wait_ge(x_in[q], landed(b, q))
                for c in range(C):
                    last = nc.vector.bn_stats(stats[:, c, :], x_sb[q][:, c, :])
                last.then_inc(stats_done, 1)
                dve.wait_ge(stats_done, b + 1)
                nc.vector.memset(wait_carrier[:, :], 0.0)
                for c in range(C):
                    last = nc.vector.bn_aggr(mean_var[:, c, :], stats[:, c, :])
                last.then_inc(aggr_done, 1)
                dve.wait_ge(aggr_done, b + 1)
                nc.vector.tensor_scalar(var_eps[:, :], mean_var[:, :, 1], EPS, None, ALU.add).then_inc(vareps_ready, 1)
                dve.wait_ge(std_ready, b + 1)
                nc.vector.reciprocal(rstd[:, :], std[:, :]).then_inc(rstd_ready, 1)
                dve.wait_ge(rstd_ready, b + 1)
                if again:
                    dve.wait_ge(hT_psum, b - 1)
                    dve.wait_ge(hhi_ready, b - 1)
                for c in range(C):
                    last = nc.vector.tensor_scalar(norm[q][:, c, :], x_sb[q][:, c, :], mean_var[:, c, 0:1],
                                                   rstd[:, c:c + 1], ALU.subtract, ALU.mult)
                last.then_inc(norm_ready, 1)

            def split_h_lo(b, q):
                dve.wait_ge(hhi_ready, b + 1)
                nc.vector.scalar_tensor_tensor(out=h_lo[q][:, :, :], in0=norm[q][:, :, :], scalar=0.0,
                                               in1=h_hi[q][:, :, :].bitcast(F32), op0=ALU.max,
                                               op1=ALU.subtract).then_inc(hlo_ready, 1)

            def split_hT_lo(b, q):
                dve.wait_ge(hThi_ready, b + 1)
                nc.vector.scalar_tensor_tensor(out=hT_lo[q][:, :], in0=bank_h[:, 0:N], scalar=0.0,
                                               in1=hT_hi[q][:, :].bitcast(F32), op0=ALU.max,
                                               op1=ALU.subtract).then_inc(hTlo_ready, 1)

            def split_adjT_lo(b, q):
                for c in range(POOL_CHUNKS, C):
                    dve.wait_ge(aThi_ready, b * C + c + 1)
                    nc.vector.tensor_tensor(aT_lo[q][:, c, :], adjT_sb[q][:, c, :], aT_hi[q][:, c, :].bitcast(F32),
                                            ALU.subtract).then_inc(aTlo_dve, 1)

            def split_gT_lo(b):
                dve.wait_ge(gThi_ready, b + 1)
                nc.vector.tensor_tensor(gT_lo[:, :], bank_gT[:, 0:N], gT_hi[:, :].bitcast(F32),
                                        ALU.subtract).then_inc(gTlo_ready, 1)

            def split_g_lo(b):
                dve.wait_ge(ghi_ready, b + 1)
                nc.vector.tensor_tensor(g_lo[:, :], bank_g[:, 0:N], g_hi[:, :].bitcast(F32),
                                        ALU.subtract).then_inc(glo_ready, 1)

            def split_sums(b, q, again):
                dve.wait_ge(ahi_ready, (b + 1) * C)
                dve.wait_ge(aThi_ready, (b + 1) * C)
                if again:
                    dve.wait_ge(sumsT_psum, b - 1)
                parts = sum_parts[q]
                s = sums[q][:, :, :].rearrange("p d c -> p c d")
                for copy in range(2):
                    last = nc.vector.tensor_copy(parts[:, :, copy, :, 0].bitcast(F32R), s)
                last.then_inc(sumhi_ready, 1)
                dve.wait_ge(sumhi_ready, b + 1)
                for copy in range(2):
                    last = nc.vector.tensor_tensor(parts[:, :, copy, :, 1], s, parts[:, :, copy, :, 0],
                                                   ALU.subtract)
                last.then_inc(sumlo_ready, 1)

            def take_best(b, q, i):
                r = ORDER[i]
                if i == 1:
                    dve.wait_ge(best_begun, b + 1)
                else:
                    dve.wait_ge(best_done, b * NBEST + i - 1)
                dve.wait_ge(prod_psum, b * NPROD + i + 1)
                if r in H_RELS:
                    op = nc.vector.scalar_tensor_tensor(out=best[q][:, :], in0=bank_p[i % NPB][:, 0:N],
                                                        scalar=c_col[:, r:r + 1], in1=best[q][:, :],
                                                        op0=ALU.add, op1=ALU.max)
                else:
                    op = nc.vector.tensor_tensor(best[q][:, :], bank_p[i % NPB][:, 0:N], best[q][:, :], ALU.max)
                op.then_inc(best_done, 1)

            def step(b, q, first, last):
                nb, nq, again = b + 1, 1 - q, not first
                if not last:
                    layernorm(nb, nq, again)
                split_gT_lo(b)
                if not last:
                    split_h_lo(nb, nq)
                take_best(b, q, 1)
                take_best(b, q, 2)
                if not last:
                    split_adjT_lo(nb, nq)
                    split_sums(nb, nq, again)
                split_g_lo(b)
                if not last:
                    split_hT_lo(nb, nq)
                for i in range(3, NPROD):
                    take_best(b, q, i)

            layernorm(0, 0, False)
            split_h_lo(0, 0)
            nc.vector.memset(c_parts[:, :, :, :, :], 0.0)
            dve.wait_ge(c_psum, 1)
            nc.vector.tensor_copy(c_col[:, :], bank_g[:, 0:R]).then_inc(c_step, 1)
            dve.wait_ge(c_step, 1)
            nc.vector.tensor_copy(c_hi[:, :], c_col[:, :]).then_inc(c_step, 1)
            dve.wait_ge(c_step, 2)
            nc.vector.tensor_tensor(c_lo[:, :], c_col[:, :], c_hi[:, :].bitcast(F32), ALU.subtract).then_inc(c_step, 1)
            dve.wait_ge(c_step, 3)
            for d, rels in enumerate((A_RELS, AT_RELS)):
                for copy, part in enumerate((c_hi[:, :].bitcast(F32), c_lo[:, :])):
                    for s in range(2):
                        last = nc.vector.tensor_copy(c_parts[:, 2 * d:2 * d + 2, copy, d, s],
                                                     part[:, rels[0]:rels[0] + 2])
            last.then_inc(c_step, 1)
            dve.wait_ge(w_hi_ready, 1)
            nc.vector.tensor_tensor(w_lo[:, :, :], w_sb[:, :, :], w_hi[:, :, :].bitcast(F32),
                                    ALU.subtract).then_inc(w_lo_ready, 1)
            split_hT_lo(0, 0)
            dve.wait_ge(crow_psum, 1)
            nc.vector.tensor_copy(c_rows[:, :, :], bank_g[0:8, :].rearrange("k (r o) -> k r o", r=4)
                                  ).then_inc(crow_ready, 1)
            split_adjT_lo(0, 0)
            split_sums(0, 0, False)
            pipeline(mybir.EngineType.DVE, step)

        @block.tensor
        def _(pe):
            def transpose_h(b, q, first):
                pe.wait_ge(norm_ready, b + 1)
                if not first:
                    pe.wait_ge(hTlo_ready, b)
                for c in range(C):
                    last = nc.tensor.transpose(bank_h[:, c * P:(c + 1) * P], norm[q][:, c, :], ident[:, :])
                last.then_inc(hT_psum, 1)

            def transpose_sums(b, q, first):
                if not first:
                    pe.wait_ge(sumsT_ready, b)
                pe.wait_ge(sumlo_ready, b + 1)
                for c in range(C):
                    last = nc.tensor.transpose(bank_s[0:8, c * P:(c + 1) * P],
                                               sum_parts[q][:, c, :, :, :].rearrange("p a b c -> p (a b c)"),
                                               ident[:, :])
                last.then_inc(sumsT_psum, 1)

            def aggregate_T(b, q, first):
                pe.wait_ge(hlo_ready, b + 1)
                if not first:
                    pe.wait_ge(gTlo_ready, b)
                for c in range(C):
                    pe.wait_ge(ahi_ready, b * C + c + 1)
                    nc.tensor.matmul(bank_gT[:, 0:N], h_hi[q][:, c, :], a_hi[q][:, c, :], start=(c == 0), stop=False)
                    nc.tensor.matmul(bank_gT[:, 0:N], h_lo[q][:, c, :], a_hi[q][:, c, :], start=False, stop=False)
                for c in range(C):
                    pe.wait_ge(alo_ready, b * C + c + 1)
                    last = nc.tensor.matmul(bank_gT[:, 0:N], h_hi[q][:, c, :], a_lo[q][:, c, :],
                                            start=False, stop=(c == C - 1))
                last.then_inc(gT_psum, 1)

            def aggregate(b, q, first):
                if not first:
                    pe.wait_ge(glo_ready, b)
                for c in range(C):
                    pe.wait_ge(aThi_ready, b * C + c + 1)
                    nc.tensor.matmul(bank_g[:, 0:N], h_hi[q][:, c, :], aT_hi[q][:, c, :], start=(c == 0), stop=False)
                    nc.tensor.matmul(bank_g[:, 0:N], h_lo[q][:, c, :], aT_hi[q][:, c, :], start=False, stop=False)
                for c in range(C):
                    if c < POOL_CHUNKS:
                        pe.wait_ge(aTlo_pool, b * POOL_CHUNKS + c + 1)
                    else:
                        pe.wait_ge(aTlo_dve, b * DVE_CHUNKS + c - POOL_CHUNKS + 1)
                    last = nc.tensor.matmul(bank_g[:, 0:N], h_hi[q][:, c, :], aT_lo[q][:, c, :],
                                            start=False, stop=(c == C - 1))
                last.then_inc(g_psum, 1)

            def product(b, q, i, first):
                r = ORDER[i]
                dst = bank_p[i % NPB][:, 0:N]
                if i == NPB:
                    pe.wait_ge(best_begun, b + 1)
                elif i > NPB:
                    pe.wait_ge(best_done, b * NBEST + i - NPB)
                elif not first:
                    pe.wait_ge(best_done, b * NBEST)
                if r in H_RELS:
                    pe.wait_ge(hTlo_ready, b + 1)
                    hi, lo = hT_hi[q], hT_lo[q]
                elif r in AT_RELS:
                    pe.wait_ge(gTlo_ready, b + 1)
                    hi, lo = gT_hi, gT_lo
                else:
                    pe.wait_ge(glo_ready, b + 1)
                    hi, lo = g_hi, g_lo
                nc.tensor.matmul(dst, w_hi[:, r, :], hi[:, :], start=True, stop=False)
                nc.tensor.matmul(dst, w_lo[:, r, :], hi[:, :], start=False, stop=False)
                last = nc.tensor.matmul(dst, w_hi[:, r, :], lo[:, :], start=False, stop=(r in H_RELS))
                if r not in H_RELS:
                    pe.wait_ge(sumsT_ready, b + 1)
                    last = nc.tensor.matmul(dst, c_rows[:, ORDER_A.index(r), :], sumsT[q][:, :],
                                            start=False, stop=True)
                last.then_inc(prod_psum, 1)

            def step(b, q, first, last):
                nb, nq = b + 1, 1 - q
                aggregate_T(b, q, first)
                if first:
                    pe.wait_ge(w_lo_ready, 1)
                for i in range(3):
                    product(b, q, i, first)
                aggregate(b, q, first)
                if first:
                    transpose_sums(0, 0, True)
                if not last:
                    transpose_h(nb, nq, False)
                product(b, q, 3, first)
                product(b, q, 4, first)
                if not last:
                    transpose_sums(nb, nq, False)
                product(b, q, 5, first)
                product(b, q, 6, first)

            pe.wait_ge(ident_ready, 1)
            transpose_h(0, 0, True)
            pe.wait_ge(wrel_in, 32)
            for r in range(R):
                last = nc.tensor.matmul(bank_g[:, r:r + 1], w_rel[:, r, :], w_edge[:, r:r + 1], start=True, stop=True)
            last.then_inc(c_psum, 1)
            pe.wait_ge(c_step, 4)
            for k in range(4):
                last = nc.tensor.transpose(bank_g[0:8, k * P:(k + 1) * P],
                                           c_parts[:, k, :, :, :].rearrange("p a b c -> p (a b c)"), ident[:, :])
            last.then_inc(crow_psum, 1)
            pe.wait_ge(crow_ready, 1)
            pipeline(mybir.EngineType.PE, step)


def kernel(x, adj, L0_gnn_W, L0_gnn_W_edges, L0_gnn_b):
    import numpy as np
    import concourse.bacc as bacc
    from concourse.bass_utils import run_bass_kernel_spmd

    batch, nodes, features = x.shape
    given = {
        "x": np.ascontiguousarray(x),
        "xT": np.ascontiguousarray(np.transpose(x, (0, 2, 1))),
        "adj": np.ascontiguousarray(adj),
        "adjT": np.ascontiguousarray(np.transpose(adj, (0, 2, 1))),
        "W": np.ascontiguousarray(L0_gnn_W),
        "W_edgesT": np.ascontiguousarray(np.transpose(L0_gnn_W_edges)),
        "biasT": np.ascontiguousarray(np.transpose(L0_gnn_b)),
    }
    nc = bacc.Bacc("TRN2", target_bir_lowering=False, num_devices=1)
    arrays, args = {}, []
    for name, a in given.items():
        arrays[f"in_{name}_dram"] = a
        args.append(nc.dram_tensor(f"in_{name}_dram", a.shape, mybir.dt.from_np(a.dtype), kind="ExternalInput").ap())
    args.append(nc.dram_tensor("out_0_dram", (batch, features, nodes), F32, kind="ExternalOutput").ap())
    gnn_kernel(nc, *args)
    r = run_bass_kernel_spmd(nc, [arrays], core_ids=[0])
    return np.ascontiguousarray(np.transpose(r.results[0]["out_0_dram"], (0, 2, 1)))
```

```python
from contextlib import ExitStack

import concourse.bass as bass
from concourse import mybir

ALU = mybir.AluOpType
ACT = mybir.ActivationFunctionType
F32 = mybir.dt.float32
F32R = mybir.dt.float32r
EPS = 1e-5
P = 128

H_RELS = (2, 5, 6)
AT_RELS = (3, 4)
A_RELS = (0, 1)
ORDER = H_RELS + AT_RELS + A_RELS
NPROD = len(ORDER)
NPB = 4
ORDER_A = A_RELS + AT_RELS
WARM_UP = 13
GROUP = 32
DVE_CHUNKS = 2


def gnn_kernel(nc: bass.Bass, x: bass.AP, xT: bass.AP, adj: bass.AP, adjT: bass.AP, W: bass.AP,
               W_rel: bass.AP, W_edges: bass.AP, biasT: bass.AP, outT: bass.AP):
    B, N, F = x.shape
    R, FE, O = W.shape
    REL = FE - F
    C = N // P
    assert F == P and O == P and N == C * P and N <= 512 and C * GROUP == P and R == NPROD and B % 2 == 0 and B >= 8

    x_dram = x.rearrange("b (c p) f -> b p c f", p=P)
    adj_dram = adj.rearrange("b (c p) m -> b p c m", p=P)
    adjT_dram = adjT.rearrange("b (c p) n -> b p c n", p=P)

    with ExitStack() as ctx:
        def sb(name, shape, dt=F32):
            return ctx.enter_context(nc.sbuf_tensor(name, shape, dt))

        def pair(name, shape, dt=F32):
            return [sb(f"{name}{i}", shape, dt) for i in range(2)]

        def bank(name):
            return ctx.enter_context(nc.psum_tensor(name, [P, 512], F32))

        def sem(name):
            return ctx.enter_context(nc.semaphore(name))

        x_sb = pair("x_sb", [P, C, F])
        xT_sb = pair("xT_sb", [P, N])
        adj_sb = pair("adj_sb", [P, C, N])
        adjT_sb = pair("adjT_sb", [P, C, N])
        h = pair("h", [P, C, F])
        h_hi = pair("h_hi", [P, C, F], F32R)
        h_lo = pair("h_lo", [P, C, F], F32R)
        hT_hi = pair("hT_hi", [P, N], F32R)
        hT_lo = pair("hT_lo", [P, N], F32R)
        a_hi = pair("a_hi", [P, C, N], F32R)
        a_lo = pair("a_lo", [P, C, N], F32R)
        aT_hi = pair("aT_hi", [P, C, N], F32R)
        aT_lo = pair("aT_lo", [P, C, N], F32R)
        x_bias = pair("x_bias", [P, N])
        sums = pair("sums", [P, 2, C])
        sum_parts = pair("sum_parts", [P, C, GROUP // 4, 2, 2], F32R)
        sumsT = pair("sumsT", [P, N], F32R)
        best = pair("best", [P, N])
        o_sb = pair("o_sb", [P, N])
        stats = sb("stats", [P, C, 6])
        mean_var = sb("mean_var", [P, C, 2])
        var_eps = sb("var_eps", [P, C])
        std = sb("std", [P, C])
        rstd = sb("rstd", [P, C])
        shift = sb("shift", [P, C])
        table_load = sb("table_load", [P, 1])
        wait_carrier = sb("wait_carrier", [P, 1])
        gT_hi = sb("gT_hi", [P, N], F32R)
        gT_lo = sb("gT_lo", [P, N], F32R)
        g_hi = sb("g_hi", [P, N], F32R)
        g_lo = sb("g_lo", [P, N], F32R)
        ident = sb("ident", [P, P])
        ident_r = sb("ident_r", [P, P], F32R)
        w_sb = sb("w_sb", [P, R, O])
        w_hi = sb("w_hi", [P, R, O], F32R)
        w_lo = sb("w_lo", [P, R, O], F32R)
        w_rel = sb("w_rel", [R * REL, O])
        w_edge = sb("w_edge", [R * REL, 1])
        blocks = sb("blocks", [R * REL, R])
        e_blocks = sb("e_blocks", [R * REL, R])
        bias_sb = sb("bias_sb", [P, N])
        c_col = sb("c_col", [P, R])
        c_hi = sb("c_hi", [P, R], F32R)
        c_lo = sb("c_lo", [P, R])
        c_parts = sb("c_parts", [P, 4, C, GROUP // 4, 2, 2])
        c_rows = sb("c_rows", [P, 4, O], F32R)

        bank_gT = bank("bank_gT")
        bank_g = bank("bank_g")
        bank_h = bank("bank_h")
        bank_s = bank("bank_s")
        bank_p = [bank(f"bank_p{i}") for i in range(NPB)]

        x0_in = [sem(f"x0_in{i}") for i in range(2)]
        x_in = [sem(f"x_in{i}") for i in range(2)]
        xT_in = [sem(f"xT_in{i}") for i in range(2)]
        adj_in = [sem(f"adj_in{i}") for i in range(2)]
        adjT_in = [sem(f"adjT_in{i}") for i in range(2)]
        stored = [sem(f"stored{i}") for i in range(2)]
        adj0_in = [sem(f"adj0_in{c}") for c in range(C)]
        adjT0_in = [sem(f"adjT0_in{c}") for c in range(C)]
        wrel_in = sem("wrel_in")
        wh_in = sem("wh_in")
        wa_in = sem("wa_in")
        bias_in = sem("bias_in")
        ident_zeroed = sem("ident_zeroed")
        ident_ready = sem("ident_ready")
        identr_ready = sem("identr_ready")
        parts_zeroed = sem("parts_zeroed")
        w_hi_ready = sem("w_hi_ready")
        wh_lo_ready = sem("wh_lo_ready")
        wa_lo_ready = sem("wa_lo_ready")
        blocks_begun = sem("blocks_begun")
        blocks_ready = sem("blocks_ready")
        e_ready = sem("e_ready")
        c_psum = sem("c_psum")
        c_step = sem("c_step")
        crow_psum = sem("crow_psum")
        crow_ready = sem("crow_ready")
        stats_done = sem("stats_done")
        aggr_done = sem("aggr_done")
        vareps_ready = sem("vareps_ready")
        std_ready = sem("std_ready")
        rstd_ready = sem("rstd_ready")
        shift_ready = sem("shift_ready")
        h_ready = sem("h_ready")
        h0_scaled = sem("h0_scaled")
        h0_ready = sem("h0_ready")
        h0hi_ready = sem("h0hi_ready")
        hhi_ready = sem("hhi_ready")
        hlo_ready = sem("hlo_ready")
        xb_ready = sem("xb_ready")
        ahi_ready = sem("ahi_ready")
        alo_dve = sem("alo_dve")
        alo_ready = sem("alo_ready")
        aThi_ready = sem("aThi_ready")
        aTlo_pool = sem("aTlo_pool")
        aTlo_dve = sem("aTlo_dve")
        hT_psum = sem("hT_psum")
        hThi_ready = sem("hThi_ready")
        hTlo_ready = sem("hTlo_ready")
        sumhi_ready = sem("sumhi_ready")
        sumlo_ready = sem("sumlo_ready")
        sumsT_psum = sem("sumsT_psum")
        sumsT_ready = sem("sumsT_ready")
        gT_psum = sem("gT_psum")
        gThi_ready = sem("gThi_ready")
        gTlo_ready = sem("gTlo_ready")
        g_psum = sem("g_psum")
        ghi_ready = sem("ghi_ready")
        glo_ready = sem("glo_ready")
        prod_psum = sem("prod_psum")
        best_begun = sem("best_begun")
        best_done = sem("best_done")
        out_ready = sem("out_ready")
        last_out_ready = sem("last_out_ready")
        last_stored = sem("last_stored")

        NBEST = NPROD - 1
        NH = len(H_RELS)
        HALF = C // 2
        HALVES = (slice(0, N // 2), slice(N // 2, N))
        LAST_BANKS = (bank_h, bank_p[(NPROD - 1) % NPB])
        POOL_CHUNKS = C - DVE_CHUNKS
        FIRST, LAST = 4, B - 2

        def landed(b, q, skipped=0):
            return (b - q) * 8 + 16 * (1 - skipped)

        def pipeline(engine_type, step):
            for b in range(2, FIRST):
                step(b, b % 2, False)
            with nc.Fori(FIRST // 2, LAST // 2, engines=[engine_type], hint_back_edge=True) as two:
                for q in range(2):
                    step(two * 2 + q, q, False)
            for b in range(LAST, B):
                step(b, b % 2, b == B - 1)

        block = ctx.enter_context(nc.Block())

        @block.sync
        def _(sp):
            def load_adj(b, q):
                sp.wait_ge(h_ready, b - 1)
                sp.wait_ge(h0_scaled, 1)
                sp.dma_start(x_sb[q][:, :, :], x_dram[b]).then_inc(x_in[q], 16)
                sp.wait_ge(alo_ready, (b - 1) * C - 1)
                sp.wait_ge(alo_dve, 1)
                sp.dma_start(adj_sb[q][:, :, :], adj_dram[b]).then_inc(adj_in[q], 16)
                sp.wait_ge(aTlo_pool, (b - 1) * POOL_CHUNKS)
                sp.wait_ge(aTlo_dve, (b - 1) * DVE_CHUNKS)
                sp.dma_start(adjT_sb[q][:, :, :], adjT_dram[b]).then_inc(adjT_in[q], 16)

            def load_xT(b, q):
                sp.wait_ge(xb_ready, b - 1)
                sp.dma_start(xT_sb[q][:, :], xT[b]).then_inc(xT_in[q], 16)

            def store(b, q):
                sp.wait_ge(out_ready, b + 1)
                sp.dma_start(outT[b], o_sb[q][:, :]).then_inc(stored[q], 16)

            def step(b, q, last):
                if not (isinstance(b, int) and b + 2 >= B):
                    load_adj(b + 2, q)
                    load_xT(b + 2, q)
                store(b - 1, 1 - q)

            for i in range(2):
                half = slice(i * HALF, (i + 1) * HALF)
                sp.dma_start(x_sb[0][:, half, :], x_dram[0][:, half, :]).then_inc(x0_in[i], 16)
            sp.dma_start(w_edge[:, :], W_edges).then_inc(wrel_in, 16)
            sp.dma_start(w_rel[:, :], W_rel).then_inc(wrel_in, 16)
            for c in range(C):
                sp.dma_start(adj_sb[0][:, c, :], adj_dram[0][:, c, :]).then_inc(adj0_in[c], 16)
            w_dram = W[:, :F, :].rearrange("r f o -> f r o")
            sp.dma_start(w_sb[:, 0:1, :], w_dram[:, 2:3, :]).then_inc(wh_in, 16)
            sp.dma_start(w_sb[:, 1:3, :], w_dram[:, 5:7, :]).then_inc(wh_in, 16)
            for c in range(C):
                if c == HALF:
                    sp.dma_start(x_sb[1][:, :, :], x_dram[1]).then_inc(x_in[1], 16)
                sp.dma_start(adjT_sb[0][:, c, :], adjT_dram[0][:, c, :]).then_inc(adjT0_in[c], 16)
            sp.dma_start(w_sb[:, 3:5, :], w_dram[:, 3:5, :]).then_inc(wa_in, 16)
            sp.dma_start(w_sb[:, 5:7, :], w_dram[:, 0:2, :]).then_inc(wa_in, 16)
            sp.dma_start(adj_sb[1][:, :, :], adj_dram[1]).then_inc(adj_in[1], 16)
            sp.dma_start(adjT_sb[1][:, :, :], adjT_dram[1]).then_inc(adjT_in[1], 16)
            load_adj(2, 0)
            sp.dma_start(bias_sb[:, :], biasT).then_inc(bias_in, 16)
            sp.dma_start(xT_sb[0][:, :], xT[0]).then_inc(xT_in[0], 16)
            sp.dma_start(xT_sb[1][:, :], xT[1]).then_inc(xT_in[1], 16)
            load_adj(3, 1)
            load_xT(2, 0)
            load_xT(3, 1)
            store(0, 0)
            pipeline(mybir.EngineType.SP, step)
            for i, nodes in enumerate(HALVES):
                sp.wait_ge(last_out_ready, i + 1)
                sp.dma_start(outT[B - 1][:, nodes], o_sb[(B - 1) % 2][:, nodes]).then_inc(last_stored, 16)
            sp.wait_ge(stored[0], 16 * (B // 2))
            sp.wait_ge(stored[1], 16 * (B // 2 - 1))
            sp.wait_ge(last_stored, 32)

        @block.gpsimd
        def _(pool):
            def split_adj_lo(b, q, again):
                if again:
                    pool.wait_ge(gT_psum, b - 1)
                for c in range(C - 1 if isinstance(b, int) and b == 0 else C):
                    pool.wait_ge(ahi_ready, b * C + c + 1)
                    nc.gpsimd.tensor_tensor(a_lo[q][:, c, :], adj_sb[q][:, c, :], a_hi[q][:, c, :].bitcast(F32),
                                            ALU.subtract).then_inc(alo_ready, 1)

            def split_adjT_lo(b, q, again):
                if again:
                    pool.wait_ge(g_psum, b - 1)
                for c in range(DVE_CHUNKS, C):
                    pool.wait_ge(aThi_ready, b * C + c + 1)
                    nc.gpsimd.tensor_tensor(aT_lo[q][:, c, :], adjT_sb[q][:, c, :], aT_hi[q][:, c, :].bitcast(F32),
                                            ALU.subtract).then_inc(aTlo_pool, 1)

            def add_bias(b, q, again):
                pool.wait_ge(xT_in[q], landed(b, q))
                if again:
                    pool.wait_ge(out_ready, b - 1)
                nc.gpsimd.tensor_tensor(x_bias[q][:, :], xT_sb[q][:, :], bias_sb[:, :], ALU.add).then_inc(xb_ready, 1)

            def finish(b, q, again):
                pool.wait_ge(xb_ready, b + 1)
                if again:
                    pool.wait_ge(stored[q], landed(b, q, 1))
                pool.wait_ge(best_done, (b + 1) * NBEST)
                nc.gpsimd.tensor_tensor(o_sb[q][:, :], best[q][:, :], x_bias[q][:, :], ALU.add).then_inc(out_ready, 1)

            def step(b, q, last):
                nb, nq = b + 1, 1 - q
                if not last:
                    split_adj_lo(nb, nq, True)
                finish(b - 1, nq, not (isinstance(b, int) and b <= 2))
                if not last:
                    add_bias(nb, nq, True)
                    split_adjT_lo(nb, nq, True)

            nc.gpsimd.memset(ident[:, :], 0.0).then_inc(ident_zeroed, 1)
            pool.wait_ge(ident_zeroed, 1)
            nc.gpsimd.affine_select(out=ident[:, :], in_=ident[:, :], compare_op=ALU.not_equal, fill=1.0,
                                    base=0, pattern=[[-1, P]], channel_multiplier=1).then_inc(ident_ready, 1)
            nc.gpsimd.memset(blocks[:, :], 1.0).then_inc(blocks_begun, 1)
            pool.wait_ge(blocks_begun, 1)
            nc.gpsimd.affine_select(out=blocks[:, :], in_=blocks[:, :], compare_op=ALU.is_ge, fill=0.0,
                                    base=0, pattern=[[-REL, R]], channel_multiplier=1).then_inc(blocks_begun, 1)
            pool.wait_ge(blocks_begun, 2)
            nc.gpsimd.affine_select(out=blocks[:, :], in_=blocks[:, :], compare_op=ALU.is_ge, fill=0.0,
                                    base=REL - 1, pattern=[[REL, R]], channel_multiplier=-1).then_inc(blocks_ready, 1)
            for q in range(2):
                nc.gpsimd.memset(sum_parts[q][:, :, :, :, :].bitcast(F32), 0.0)
                last = nc.gpsimd.memset(sumsT[q][:, :].bitcast(F32), 0.0)
            last.then_inc(parts_zeroed, 1)
            split_adj_lo(0, 0, False)
            split_adjT_lo(0, 0, False)
            pool.wait_ge(w_hi_ready, 2)
            nc.gpsimd.tensor_tensor(w_lo[:, NH:, :], w_sb[:, NH:, :], w_hi[:, NH:, :].bitcast(F32),
                                    ALU.subtract).then_inc(wa_lo_ready, 1)
            split_adj_lo(1, 1, False)
            split_adjT_lo(1, 1, False)
            pool.wait_ge(bias_in, 16)
            add_bias(0, 0, False)
            add_bias(1, 1, False)
            step(1, 1, False)
            pipeline(mybir.EngineType.Pool, step)

        @block.scalar
        def _(act):
            def std_of(b):
                act.wait_ge(vareps_ready, b + 1)
                nc.scalar.activation(std[:, :], var_eps[:, :], ACT.Sqrt).then_inc(std_ready, 1)

            def split_adj(b, q, chunks, again):
                for c in chunks:
                    if isinstance(b, int) and b == 0:
                        act.wait_ge(adj0_in[c], 16)
                    elif c == 0:
                        act.wait_ge(adj_in[q], landed(b, q, 1 - q))
                    if again and c == 0:
                        act.wait_ge(gT_psum, b - 1)
                        act.wait_ge(sumlo_ready, b - 1)
                    nc.scalar.activation(a_hi[q][:, c, :], adj_sb[q][:, c, :], ACT.Copy,
                                         accum_out=sums[q][:, 0, c:c + 1]).then_inc(ahi_ready, 1)

            def split_adjT(b, q, chunks, again):
                for c in chunks:
                    if isinstance(b, int) and b == 0:
                        act.wait_ge(adjT0_in[c], 16)
                    elif c == 0:
                        act.wait_ge(adjT_in[q], landed(b, q, 1 - q))
                        if again:
                            act.wait_ge(g_psum, b - 1)
                    nc.scalar.activation(aT_hi[q][:, c, :], adjT_sb[q][:, c, :], ACT.Copy,
                                         accum_out=sums[q][:, 1, c:c + 1]).then_inc(aThi_ready, 1)

            def make_h(b, q, again):
                act.wait_ge(shift_ready, b + 1)
                if again:
                    act.wait_ge(hT_psum, b - 1)
                    act.wait_ge(hlo_ready, b - 1)
                for c in range(C):
                    last = nc.scalar.activation(h[q][:, c, :], x_sb[q][:, c, :], ACT.Relu,
                                                bias=shift[:, c:c + 1], scale=rstd[:, c:c + 1])
                last.then_inc(h_ready, 1)

            def split_h(b, q, again):
                act.wait_ge(h_ready, b + 1)
                if again:
                    act.wait_ge(g_psum, b - 1)
                nc.scalar.activation(h_hi[q][:, :, :], h[q][:, :, :], ACT.Copy).then_inc(hhi_ready, 1)

            def split_hT(b, q, again):
                act.wait_ge(hT_psum, b + 1)
                if again:
                    act.wait_ge(prod_psum, (b - 2) * NPROD + len(H_RELS))
                nc.scalar.activation(hT_hi[q][:, :], bank_h[:, 0:N], ACT.Copy).then_inc(hThi_ready, 1)

            def split_gT(b, first):
                act.wait_ge(gT_psum, b + 1)
                if not first:
                    act.wait_ge(prod_psum, b * NPROD - len(A_RELS))
                nc.scalar.activation(gT_hi[:, :], bank_gT[:, 0:N], ACT.Copy).then_inc(gThi_ready, 1)

            def split_g(b, first):
                act.wait_ge(g_psum, b + 1)
                if not first:
                    act.wait_ge(prod_psum, b * NPROD)
                nc.scalar.activation(g_hi[:, :], bank_g[:, 0:N], ACT.Copy).then_inc(ghi_ready, 1)

            def begin_best(b, q, again):
                r = ORDER[0]
                act.wait_ge(prod_psum, b * NPROD + 1)
                if again:
                    act.wait_ge(out_ready, b - 1)
                nc.scalar.activation(best[q][:, :], bank_p[0][:, 0:N], ACT.Identity,
                                     bias=c_col[:, r:r + 1]).then_inc(best_begun, 1)

            def copy_sumsT(b, q, again):
                act.wait_ge(sumsT_psum, b + 1)
                if again:
                    act.wait_ge(prod_psum, (b - 1) * NPROD)
                for c in range(C):
                    rows = slice(c * GROUP, (c + 1) * GROUP)
                    last = nc.scalar.activation(sumsT[q][rows, c * P:(c + 1) * P], bank_s[rows, 0:P], ACT.Copy)
                last.then_inc(sumsT_ready, 1)

            def step(b, q, last):
                nb, nq = b + 1, 1 - q
                if not last:
                    split_adj(nb, nq, range(C), True)
                    split_adjT(nb, nq, range(0, 2), True)
                    std_of(nb)
                split_gT(b, False)
                begin_best(b, q, not (isinstance(b, int) and b < 2))
                if not last:
                    make_h(nb, nq, True)
                copy_sumsT(b, q, not (isinstance(b, int) and b < 2))
                if not last:
                    split_h(nb, nq, True)
                split_g(b, False)
                if not last:
                    split_adjT(nb, nq, range(2, 3), True)
                    split_hT(nb, nq, True)
                    split_adjT(nb, nq, range(3, C), True)

            act.wait_ge(ident_ready, 1)
            nc.scalar.activation(table_load[:, :], ident[:, 0:1], ACT.Sqrt)
            std_of(0)
            split_adj(0, 0, range(0, 1), False)
            act.wait_ge(shift_ready, 1)
            for c in range(HALF):
                last = nc.scalar.activation(h[0][:, c, :], x_sb[0][:, c, :], ACT.Relu,
                                            bias=shift[:, c:c + 1], scale=rstd[:, c:c + 1])
            last.then_inc(h_ready, 1)
            split_adj(0, 0, range(1, C), False)
            split_hT(0, 0, False)
            act.wait_ge(wh_in, 32)
            nc.scalar.activation(w_hi[:, :NH, :], w_sb[:, :NH, :], ACT.Copy).then_inc(w_hi_ready, 1)
            split_adjT(0, 0, range(C), False)
            split_gT(0, True)
            std_of(1)
            act.wait_ge(wa_in, 32)
            nc.scalar.activation(w_hi[:, NH:, :], w_sb[:, NH:, :], ACT.Copy).then_inc(w_hi_ready, 1)
            act.wait_ge(c_step, 1)
            begin_best(0, 0, False)
            make_h(1, 1, False)
            split_h(1, 1, False)
            copy_sumsT(0, 0, False)
            split_g(0, True)
            split_adj(1, 1, range(C), False)
            split_hT(1, 1, False)
            std_of(2)
            split_adjT(1, 1, range(C), False)
            split_gT(1, False)
            begin_best(1, 1, False)
            make_h(2, 0, True)
            copy_sumsT(1, 1, False)
            split_adj(2, 0, range(C), True)
            split_g(1, False)
            split_h(2, 0, True)
            split_hT(2, 0, True)
            split_adjT(2, 0, range(C), True)
            pipeline(mybir.EngineType.Activation, step)

        @block.vector
        def _(dve):
            def variance(b, q):
                if isinstance(b, int) and b == 0:
                    for c in range(C):
                        if c % HALF == 0:
                            dve.wait_ge(x0_in[c // HALF], 16)
                        last = nc.vector.bn_stats(stats[:, c, :], x_sb[0][:, c, :])
                else:
                    dve.wait_ge(x_in[q], landed(b, q, 1 - q))
                    for c in range(C):
                        last = nc.vector.bn_stats(stats[:, c, :], x_sb[q][:, c, :])
                last.then_inc(stats_done, 1)
                dve.wait_ge(stats_done, b + 1)
                nc.vector.memset(wait_carrier[:, :], 0.0)
                for c in range(C):
                    last = nc.vector.bn_aggr(mean_var[:, c, :], stats[:, c, :])
                last.then_inc(aggr_done, 1)
                dve.wait_ge(aggr_done, b + 1)
                nc.vector.tensor_scalar(var_eps[:, :], mean_var[:, :, 1], EPS, None, ALU.add).then_inc(vareps_ready, 1)

            def scale_and_shift(b, first):
                dve.wait_ge(std_ready, b + 1)
                if not first:
                    dve.wait_ge(h_ready, b)
                nc.vector.reciprocal(rstd[:, :], std[:, :]).then_inc(rstd_ready, 1)
                dve.wait_ge(rstd_ready, b + 1)
                nc.vector.scalar_tensor_tensor(out=shift[:, :], in0=mean_var[:, :, 0], scalar=-1.0, in1=rstd[:, :],
                                               op0=ALU.mult, op1=ALU.mult).then_inc(shift_ready, 1)

            def split_h_lo(b, q):
                dve.wait_ge(hhi_ready, b)
                nc.vector.tensor_tensor(h_lo[q][:, :, :], h[q][:, :, :], h_hi[q][:, :, :].bitcast(F32),
                                        ALU.subtract).then_inc(hlo_ready, 1)

            def split_hT_lo(b, q):
                dve.wait_ge(hThi_ready, b + 1)
                nc.vector.tensor_tensor(hT_lo[q][:, :], bank_h[:, 0:N], hT_hi[q][:, :].bitcast(F32),
                                        ALU.subtract).then_inc(hTlo_ready, 1)

            def split_adjT_lo(b, q):
                for c in range(DVE_CHUNKS):
                    dve.wait_ge(aThi_ready, b * C + c + 1)
                    nc.vector.tensor_tensor(aT_lo[q][:, c, :], adjT_sb[q][:, c, :], aT_hi[q][:, c, :].bitcast(F32),
                                            ALU.subtract).then_inc(aTlo_dve, 1)

            def split_gT_lo(b):
                dve.wait_ge(gThi_ready, b + 1)
                nc.vector.tensor_tensor(gT_lo[:, :], bank_gT[:, 0:N], gT_hi[:, :].bitcast(F32),
                                        ALU.subtract).then_inc(gTlo_ready, 1)

            def split_g_lo(b):
                dve.wait_ge(ghi_ready, b + 1)
                nc.vector.tensor_tensor(g_lo[:, :], bank_g[:, 0:N], g_hi[:, :].bitcast(F32),
                                        ALU.subtract).then_inc(glo_ready, 1)

            def split_sums(b, q, again):
                dve.wait_ge(ahi_ready, (b + 1) * C)
                dve.wait_ge(aThi_ready, (b + 1) * C)
                if again:
                    dve.wait_ge(sumsT_psum, b - 1)
                parts = sum_parts[q]
                s = sums[q][:, :, :].rearrange("p d c -> p c d")
                for copy in range(2):
                    last = nc.vector.tensor_copy(parts[:, :, copy, :, 0], s)
                last.then_inc(sumhi_ready, 1)
                dve.wait_ge(sumhi_ready, b + 1)
                for copy in range(2):
                    last = nc.vector.tensor_tensor(parts[:, :, copy, :, 1], s, parts[:, :, copy, :, 0].bitcast(F32),
                                                   ALU.subtract)
                last.then_inc(sumlo_ready, 1)

            def take_best(b, q, i):
                r = ORDER[i]
                if i == 1:
                    dve.wait_ge(best_begun, b + 1)
                else:
                    dve.wait_ge(best_done, b * NBEST + i - 1)
                dve.wait_ge(prod_psum, b * NPROD + i + 1)
                if r in H_RELS:
                    op = nc.vector.scalar_tensor_tensor(out=best[q][:, :], in0=bank_p[i % NPB][:, 0:N],
                                                        scalar=c_col[:, r:r + 1], in1=best[q][:, :],
                                                        op0=ALU.add, op1=ALU.max)
                else:
                    op = nc.vector.tensor_tensor(best[q][:, :], bank_p[i % NPB][:, 0:N], best[q][:, :], ALU.max)
                op.then_inc(best_done, 1)

            def step(b, q, last):
                nb, nq = b + 1, 1 - q
                if not last:
                    scale_and_shift(nb, False)
                    split_adjT_lo(nb, nq)
                split_gT_lo(b)
                take_best(b, q, 1)
                take_best(b, q, 2)
                if not last:
                    split_h_lo(nb, nq)
                split_g_lo(b)
                take_best(b, q, 3)
                if not last:
                    split_hT_lo(nb, nq)
                take_best(b, q, 4)
                take_best(b, q, 5)
                if not last:
                    split_sums(nb, nq, True)
                if not (isinstance(b, int) and b + 2 >= B):
                    variance(b + 2, q)
                if not last:
                    take_best(b, q, NPROD - 1)

            dve.wait_ge(ident_ready, 1)
            nc.vector.tensor_copy(ident_r[:, :], ident[:, :]).then_inc(identr_ready, 1)
            nc.vector.memset(c_parts[:, :, :, :, :, :], 0.0)
            variance(0, 0)
            scale_and_shift(0, True)
            dve.wait_ge(blocks_ready, 1)
            dve.wait_ge(wrel_in, 32)
            nc.vector.tensor_scalar(e_blocks[:, :], blocks[:, :], w_edge[:, :], None, ALU.mult).then_inc(e_ready, 1)
            dve.wait_ge(shift_ready, 1)
            for c in range(HALF, C):
                last = nc.vector.tensor_scalar(h[0][:, c, :], x_sb[0][:, c, :], rstd[:, c:c + 1], shift[:, c:c + 1],
                                               ALU.mult, ALU.add)
            last.then_inc(h0_scaled, 1)
            dve.wait_ge(h0_scaled, 1)
            nc.vector.tensor_scalar(h[0][:, HALF:, :], h[0][:, HALF:, :], 0.0, None, ALU.max).then_inc(h0_ready, 1)
            dve.wait_ge(h_ready, 1)
            nc.vector.tensor_copy(h_hi[0][:, :HALF, :], h[0][:, :HALF, :])
            dve.wait_ge(h0_ready, 1)
            nc.vector.tensor_copy(h_hi[0][:, HALF:, :], h[0][:, HALF:, :]).then_inc(h0hi_ready, 1)
            dve.wait_ge(h0hi_ready, 1)
            nc.vector.tensor_tensor(h_lo[0][:, :, :], h[0][:, :, :], h_hi[0][:, :, :].bitcast(F32),
                                    ALU.subtract).then_inc(hlo_ready, 1)
            dve.wait_ge(c_psum, 1)
            nc.vector.tensor_copy(c_col[:, :], bank_g[:, 0:R]).then_inc(c_step, 1)
            dve.wait_ge(c_step, 1)
            nc.vector.tensor_copy(c_hi[:, :], c_col[:, :]).then_inc(c_step, 1)
            dve.wait_ge(c_step, 2)
            nc.vector.tensor_tensor(c_lo[:, :], c_col[:, :], c_hi[:, :].bitcast(F32), ALU.subtract).then_inc(c_step, 1)
            dve.wait_ge(ahi_ready, C)
            nc.vector.tensor_tensor(a_lo[0][:, C - 1, :], adj_sb[0][:, C - 1, :], a_hi[0][:, C - 1, :].bitcast(F32),
                                    ALU.subtract).then_inc(alo_dve, 1)
            split_hT_lo(0, 0)
            dve.wait_ge(w_hi_ready, 1)
            nc.vector.tensor_tensor(w_lo[:, :NH, :], w_sb[:, :NH, :], w_hi[:, :NH, :].bitcast(F32),
                                    ALU.subtract).then_inc(wh_lo_ready, 1)
            dve.wait_ge(c_step, 3)
            for d, rels in enumerate((A_RELS, AT_RELS)):
                for copy, part in enumerate((c_hi[:, :].bitcast(F32), c_lo[:, :])):
                    for s in range(2):
                        last = nc.vector.tensor_copy(
                            c_parts[:, 2 * d:2 * d + 2, :, copy, d, s],
                            part[:, rels[0]:rels[0] + 2].unsqueeze(2).to_broadcast([P, 2, C]))
            last.then_inc(c_step, 1)
            variance(1, 1)
            split_adjT_lo(0, 0)
            scale_and_shift(1, False)
            split_gT_lo(0)
            dve.wait_ge(crow_psum, 1)
            nc.vector.tensor_copy(c_rows[:, :, :], bank_p[NPB - 1][:, :].rearrange("k (r o) -> k r o", r=4)
                                  ).then_inc(crow_ready, 1)
            dve.wait_ge(parts_zeroed, 1)
            split_sums(0, 0, False)
            take_best(0, 0, 1)
            take_best(0, 0, 2)
            split_h_lo(1, 1)
            split_g_lo(0)
            take_best(0, 0, 3)
            variance(2, 0)
            split_hT_lo(1, 1)
            take_best(0, 0, 4)
            scale_and_shift(2, False)
            split_adjT_lo(1, 1)
            split_sums(1, 1, False)
            take_best(0, 0, 5)
            take_best(0, 0, 6)
            split_gT_lo(1)
            take_best(1, 1, 1)
            take_best(1, 1, 2)
            variance(3, 1)
            split_g_lo(1)
            take_best(1, 1, 3)
            split_h_lo(2, 0)
            split_hT_lo(2, 0)
            take_best(1, 1, 4)
            take_best(1, 1, 5)
            split_adjT_lo(2, 0)
            split_sums(2, 0, True)
            take_best(1, 1, 6)
            pipeline(mybir.EngineType.DVE, step)
            b, q = B - 1, (B - 1) % 2
            dve.wait_ge(xb_ready, B)
            dve.wait_ge(stored[q], landed(b, q, 1))
            dve.wait_ge(best_done, B * NBEST - 1)
            for i, nodes in enumerate(HALVES):
                dve.wait_ge(prod_psum, B * NPROD + i)
                nc.vector.tensor_tensor(best[q][:, nodes], LAST_BANKS[i][:, nodes], best[q][:, nodes],
                                        ALU.max).then_inc(best_done, 1)
                dve.wait_ge(best_done, B * NBEST + i)
                nc.vector.tensor_tensor(o_sb[q][:, nodes], best[q][:, nodes], x_bias[q][:, nodes],
                                        ALU.add).then_inc(last_out_ready, 1)

        @block.tensor
        def _(pe):
            def transpose_h(b, q, first):
                pe.wait_ge(h_ready, b + 1)
                if first:
                    pe.wait_ge(h0_ready, 1)
                else:
                    pe.wait_ge(hTlo_ready, b)
                for c in range(C):
                    last = nc.tensor.transpose(bank_h[:, c * P:(c + 1) * P], h[q][:, c, :], ident[:, :])
                last.then_inc(hT_psum, 1)

            def transpose_sums(b, q, first):
                if not first:
                    pe.wait_ge(sumsT_ready, b)
                pe.wait_ge(sumlo_ready, b + 1)
                nc.tensor.matmul(bank_s[:, 0:P], sum_parts[q][:, :, :, :, :].rearrange("p e a b c -> p (e a b c)"),
                                 ident_r[:, :], start=True, stop=True).then_inc(sumsT_psum, 1)

            def aggregate_T(b, q, first):
                pe.wait_ge(hlo_ready, b + 1)
                if not first:
                    pe.wait_ge(gTlo_ready, b)
                for c in range(C):
                    pe.wait_ge(ahi_ready, b * C + c + 1)
                    nc.tensor.matmul(bank_gT[:, 0:N], h_hi[q][:, c, :], a_hi[q][:, c, :], start=(c == 0), stop=False)
                    nc.tensor.matmul(bank_gT[:, 0:N], h_lo[q][:, c, :], a_hi[q][:, c, :], start=False, stop=False)
                for c in range(C):
                    if not first:
                        pe.wait_ge(alo_ready, b * C + c)
                    elif c < C - 1:
                        pe.wait_ge(alo_ready, c + 1)
                    else:
                        pe.wait_ge(alo_dve, 1)
                    last = nc.tensor.matmul(bank_gT[:, 0:N], h_hi[q][:, c, :], a_lo[q][:, c, :],
                                            start=False, stop=(c == C - 1))
                last.then_inc(gT_psum, 1)

            def aggregate(b, q, first):
                if not first:
                    pe.wait_ge(glo_ready, b)
                for c in range(C):
                    pe.wait_ge(aThi_ready, b * C + c + 1)
                    nc.tensor.matmul(bank_g[:, 0:N], h_hi[q][:, c, :], aT_hi[q][:, c, :], start=(c == 0), stop=False)
                    nc.tensor.matmul(bank_g[:, 0:N], h_lo[q][:, c, :], aT_hi[q][:, c, :], start=False, stop=False)
                for c in range(C):
                    if c < DVE_CHUNKS:
                        pe.wait_ge(aTlo_dve, b * DVE_CHUNKS + c + 1)
                    else:
                        pe.wait_ge(aTlo_pool, b * POOL_CHUNKS + c - DVE_CHUNKS + 1)
                    last = nc.tensor.matmul(bank_g[:, 0:N], h_hi[q][:, c, :], aT_lo[q][:, c, :],
                                            start=False, stop=(c == C - 1))
                last.then_inc(g_psum, 1)

            def product(b, q, i, first, nodes=slice(0, N), bank=None):
                r = ORDER[i]
                dst = (bank or bank_p[i % NPB])[:, nodes]
                if i == NPB:
                    pe.wait_ge(best_begun, b + 1)
                elif i > NPB:
                    pe.wait_ge(best_done, b * NBEST + i - NPB)
                elif not first:
                    pe.wait_ge(best_done, (b - 1) * NBEST + (i + NPB if i + NPB < NPROD else i))
                if r in H_RELS:
                    pe.wait_ge(hTlo_ready, b + 1)
                    hi, lo = hT_hi[q], hT_lo[q]
                elif r in AT_RELS:
                    pe.wait_ge(gTlo_ready, b + 1)
                    hi, lo = gT_hi, gT_lo
                else:
                    pe.wait_ge(glo_ready, b + 1)
                    hi, lo = g_hi, g_lo
                nc.tensor.matmul(dst, w_hi[:, i, :], hi[:, nodes], start=True, stop=False)
                nc.tensor.matmul(dst, w_lo[:, i, :], hi[:, nodes], start=False, stop=False)
                last = nc.tensor.matmul(dst, w_hi[:, i, :], lo[:, nodes], start=False, stop=(r in H_RELS))
                if r not in H_RELS:
                    pe.wait_ge(sumsT_ready, b + 1)
                    last = nc.tensor.matmul(dst, c_rows[:, ORDER_A.index(r), :], sumsT[q][:, nodes],
                                            start=False, stop=True)
                last.then_inc(prod_psum, 1)

            def step(b, q, last):
                nb, nq = b + 1, 1 - q
                aggregate_T(b, q, False)
                for i in range(NH):
                    product(b, q, i, False)
                transpose_sums(b, q, False)
                aggregate(b, q, False)
                if not last:
                    transpose_h(nb, nq, False)
                for i in range(NH, NPROD - 1):
                    product(b, q, i, False)
                if last:
                    for nodes, bank in zip(HALVES, LAST_BANKS):
                        product(b, q, NPROD - 1, False, nodes, bank)
                else:
                    product(b, q, NPROD - 1, False)

            pe.wait_ge(ident_ready, 1)
            for _ in range(WARM_UP):
                nc.tensor.matmul(bank_p[0][:, 0:P], ident[:, :], ident[:, :], start=True, stop=True)
            transpose_h(0, 0, True)
            pe.wait_ge(e_ready, 1)
            nc.tensor.matmul(bank_g[:, 0:R], w_rel[:, :], e_blocks[:, :], start=True, stop=True).then_inc(c_psum, 1)
            aggregate_T(0, 0, True)
            pe.wait_ge(wh_lo_ready, 1)
            for i in range(NH):
                product(0, 0, i, True)
            pe.wait_ge(c_step, 4)
            for k in range(4):
                turn = nc.tensor.transpose(bank_p[NPB - 1][:, k * P:(k + 1) * P],
                                           c_parts[:, k, :, :, :, :].rearrange("p e a b c -> p (e a b c)"),
                                           ident[:, :])
            turn.then_inc(crow_psum, 1)
            aggregate(0, 0, True)
            pe.wait_ge(identr_ready, 1)
            transpose_sums(0, 0, True)
            transpose_h(1, 1, False)
            pe.wait_ge(wa_lo_ready, 1)
            pe.wait_ge(crow_ready, 1)
            for i in range(NH, NPROD):
                product(0, 0, i, True)
            step(1, 1, False)
            pipeline(mybir.EngineType.PE, step)


def kernel(x, adj, L0_gnn_W, L0_gnn_W_edges, L0_gnn_b):
    import numpy as np
    import concourse.bacc as bacc
    from concourse.bass_utils import run_bass_kernel_spmd

    batch, nodes, features = x.shape
    given = {
        "x": np.ascontiguousarray(x),
        "xT": np.ascontiguousarray(np.transpose(x, (0, 2, 1))),
        "adj": np.ascontiguousarray(adj),
        "adjT": np.ascontiguousarray(np.transpose(adj, (0, 2, 1))),
        "W": np.ascontiguousarray(L0_gnn_W),
        "W_rel": np.ascontiguousarray(L0_gnn_W[:, features:, :]).reshape(-1, L0_gnn_W.shape[2]),
        "W_edges": np.ascontiguousarray(L0_gnn_W_edges).reshape(-1, 1),
        "biasT": np.ascontiguousarray(np.transpose(L0_gnn_b)),
    }
    nc = bacc.Bacc("TRN2", target_bir_lowering=False, num_devices=1)
    arrays, args = {}, []
    for name, a in given.items():
        arrays[f"in_{name}_dram"] = a
        args.append(nc.dram_tensor(f"in_{name}_dram", a.shape, mybir.dt.from_np(a.dtype), kind="ExternalInput").ap())
    args.append(nc.dram_tensor("out_0_dram", (batch, features, nodes), F32, kind="ExternalOutput").ap())
    gnn_kernel(nc, *args)
    r = run_bass_kernel_spmd(nc, [arrays], core_ids=[0])
    return np.ascontiguousarray(np.transpose(r.results[0]["out_0_dram"], (0, 2, 1)))
```
